# Optimizing a Trainium2 kernel written in Bass

```python
import numpy as np
import jax
import jax.numpy as jnp

def _softmax(x, axis=-1):
    return jax.nn.softmax(x, axis=axis)

def _gelu(x):
    return jax.nn.gelu(x, approximate=True)

def _silu(x):
    return jax.nn.silu(x)

def _sigmoid(x):
    return jax.nn.sigmoid(x)

def _layernorm(x, axis=-1, eps=1e-05):
    m = jnp.mean(x, axis=axis, keepdims=True)
    v = jnp.var(x, axis=axis, keepdims=True)
    return (x - m) / jnp.sqrt(v + eps)

def _scatter_add(tgt, idx, src, axis=0):
    return tgt.at[idx].add(src)

def _segment_sum(src, seg, n):
    return jax.ops.segment_sum(src, seg, n)
kernel_name = 'mk_vit_tower_d1_tok_img768_r4_f0a727'

def setup_inputs(seed: int=0):
    np.random.seed(seed)
    _w = jnp.asarray

    def _rec_inputs():
        import jax
        import jax.numpy as jnp
        _rk = jax.random.key(seed)
        x = -0.000356955 + 1 * jax.random.normal(jax.random.fold_in(_rk, 1), (64, 3, 224, 224), jnp.float32)
        return x
    x = _rec_inputs()

    def _L0_tok_setup():
        import jax, jax.numpy as jnp
        import numpy as np
        C, H, W = (3, 224, 224)
        P = 14
        PS = H // P
        PATCH_DIM = C * PS * PS
        HIDDEN = 192

        def patchify(images):
            n = images.shape[0]
            x = images.reshape(n, C, P, PS, P, PS)
            x = x.transpose(0, 2, 4, 1, 3, 5)
            return x.reshape(n, P * P, PATCH_DIM)
        key = jax.random.key(seed)
        k1, k2, k3 = jax.random.split(key, 3)
        images = jax.random.normal(k1, (128, C, H, W), dtype=jnp.float32)
        bound = 1.0 / np.sqrt(PATCH_DIM)
        W_lin = jax.random.uniform(k2, (HIDDEN, PATCH_DIM), minval=-bound, maxval=bound, dtype=jnp.float32)
        b_lin = jax.random.uniform(k3, (HIDDEN,), minval=-bound, maxval=bound, dtype=jnp.float32)
        cls_token = jnp.ones((1, HIDDEN), dtype=jnp.float32)
        return {'images': images, 'W_lin': W_lin, 'b_lin': b_lin, 'cls_token': cls_token}
    _L0_tok_all = _L0_tok_setup()
    _L0_tok_in = {k: v for k, v in _L0_tok_all.items() if k in ('W_lin', 'b_lin', 'cls_token')}
    del _L0_tok_all

    def _L0_attn_setup():
        import jax, jax.numpy as jnp
        import numpy as np
        B, N, C = (8, 256, 192)
        H = 12
        D = C // H
        SCALE = D ** (-0.5)
        EPS = 1e-05

        def _layer_norm(x):
            mean = x.mean(-1, keepdims=True)
            var = ((x - mean) ** 2).mean(-1, keepdims=True)
            return (x - mean) / jnp.sqrt(var + EPS)
        key = jax.random.key(seed)
        k1, k2, k3 = jax.random.split(key, 3)
        x = jax.random.normal(k1, (B, N, C), dtype=jnp.float32)
        qkv_weight = jax.random.normal(k2, (3 * C, C), dtype=jnp.float32) * C ** (-0.5)
        proj_weight = jax.random.normal(k3, (C, C), dtype=jnp.float32) * C ** (-0.5)
        return {'x': x, 'qkv_weight': qkv_weight, 'proj_weight': proj_weight}
    _L0_attn_all = _L0_attn_setup()
    _L0_attn_in = {k: v for k, v in _L0_attn_all.items() if k in ('qkv_weight', 'proj_weight')}
    del _L0_attn_all

    def _L0_ffn_setup():
        import jax, jax.numpy as jnp
        import numpy as np
        from jax import lax
        DIM = 192
        INTER = 128
        E = 8
        G = 4
        TOPK_G = 2
        TOPK = 2
        ROUTE_SCALE = 1.0

        def _gate(x2, gate_weight, gate_bias):
            T = x2.shape[0]
            scores = jax.nn.sigmoid(x2 @ gate_weight.T)
            s = scores + gate_bias
            sv = s.reshape(T, G, E // G)
            top2, _ = lax.top_k(sv, 2)
            group_scores = top2.sum(-1)
            _, gidx = lax.top_k(group_scores, TOPK_G)
            gmask = jnp.zeros((T, G), bool).at[jnp.arange(T)[:, None], gidx].set(True)
            masked = jnp.where(gmask[:, :, None], sv, -jnp.inf).reshape(T, E)
            _, idx = lax.top_k(masked, TOPK)
            w = jnp.take_along_axis(scores, idx, axis=1)
            w = w / (w.sum(-1, keepdims=True) + 1e-06) * ROUTE_SCALE
            return (w, idx)
        key = jax.random.key(seed)
        ks = jax.random.split(key, 9)
        s = 1.0 / np.sqrt(DIM)
        si = 1.0 / np.sqrt(INTER)
        return {'x': jax.random.normal(ks[0], (4, 1024, DIM), jnp.float32), 'gate_weight': jax.random.uniform(ks[1], (E, DIM), jnp.float32, -s, s), 'gate_bias': jnp.zeros((E,), jnp.float32), 'w1': jax.random.uniform(ks[2], (E, INTER, DIM), jnp.float32, -s, s), 'w2': jax.random.uniform(ks[3], (E, DIM, INTER), jnp.float32, -si, si), 'w3': jax.random.uniform(ks[4], (E, INTER, DIM), jnp.float32, -s, s), 'sw1': jax.random.uniform(ks[5], (INTER, DIM), jnp.float32, -s, s), 'sw2': jax.random.uniform(ks[6], (DIM, INTER), jnp.float32, -si, si), 'sw3': jax.random.uniform(ks[7], (INTER, DIM), jnp.float32, -s, s)}
    _L0_ffn_all = _L0_ffn_setup()
    _L0_ffn_in = {k: v for k, v in _L0_ffn_all.items() if k in ('gate_weight', 'gate_bias', 'w1', 'w2', 'w3', 'sw1', 'sw2', 'sw3')}
    del _L0_ffn_all
    return {'x': x, 'L0_tok_W_lin': _L0_tok_in['W_lin'], 'L0_tok_b_lin': _L0_tok_in['b_lin'], 'L0_tok_cls_token': _L0_tok_in['cls_token'], 'L0_attn_qkv_weight': _L0_attn_in['qkv_weight'], 'L0_attn_proj_weight': _L0_attn_in['proj_weight'], 'L0_ffn_gate_weight': _L0_ffn_in['gate_weight'], 'L0_ffn_gate_bias': _L0_ffn_in['gate_bias'], 'L0_ffn_w1': _L0_ffn_in['w1'], 'L0_ffn_w2': _L0_ffn_in['w2'], 'L0_ffn_w3': _L0_ffn_in['w3'], 'L0_ffn_sw1': _L0_ffn_in['sw1'], 'L0_ffn_sw2': _L0_ffn_in['sw2'], 'L0_ffn_sw3': _L0_ffn_in['sw3']}

def reference(x, L0_tok_W_lin, L0_tok_b_lin, L0_tok_cls_token, L0_attn_qkv_weight, L0_attn_proj_weight, L0_ffn_gate_weight, L0_ffn_gate_bias, L0_ffn_w1, L0_ffn_w2, L0_ffn_w3, L0_ffn_sw1, L0_ffn_sw2, L0_ffn_sw3):
    import jax
    import jax.numpy as jnp

    def _L0_tok_ref(images, W_lin, b_lin, cls_token):
        import jax, jax.numpy as jnp
        import numpy as np
        C, H, W = (3, 224, 224)
        P = 14
        PS = H // P
        PATCH_DIM = C * PS * PS
        HIDDEN = 192

        def patchify(images):
            n = images.shape[0]
            x = images.reshape(n, C, P, PS, P, PS)
            x = x.transpose(0, 2, 4, 1, 3, 5)
            return x.reshape(n, P * P, PATCH_DIM)
        patches = patchify(images)
        hidden = jnp.einsum('npd,hd->nph', patches, W_lin) + b_lin
        n = images.shape[0]
        cls = jnp.broadcast_to(cls_token[None], (n, 1, HIDDEN))
        return jnp.concatenate([cls, hidden], axis=1)

    def _L0_attn_ref(x, qkv_weight, proj_weight):
        import jax, jax.numpy as jnp
        import numpy as np
        B, N, C = (8, 256, 192)
        H = 12
        D = C // H
        SCALE = D ** (-0.5)
        EPS = 1e-05

        def _layer_norm(x):
            mean = x.mean(-1, keepdims=True)
            var = ((x - mean) ** 2).mean(-1, keepdims=True)
            return (x - mean) / jnp.sqrt(var + EPS)
        Bx, Nx, Cx = x.shape
        qkv = x @ qkv_weight.T
        qkv = qkv.reshape(Bx, Nx, 3, H, D).transpose(2, 0, 3, 1, 4)
        q, k, v = (qkv[0], qkv[1], qkv[2])
        q = _layer_norm(q) * SCALE
        k = _layer_norm(k)
        attn = jnp.einsum('bhnd,bhmd->bhnm', q, k)
        attn = jax.nn.softmax(attn, axis=-1)
        out = jnp.einsum('bhnm,bhmd->bhnd', attn, v)
        out = out.transpose(0, 2, 1, 3).reshape(Bx, Nx, Cx)
        return out @ proj_weight.T

    def _L0_ffn_ref(x, gate_weight, gate_bias, w1, w2, w3, sw1, sw2, sw3):
        import jax, jax.numpy as jnp
        import numpy as np
        from jax import lax
        DIM = 192
        INTER = 128
        E = 8
        G = 4
        TOPK_G = 2
        TOPK = 2
        ROUTE_SCALE = 1.0

        def _gate(x2, gate_weight, gate_bias):
            T = x2.shape[0]
            scores = jax.nn.sigmoid(x2 @ gate_weight.T)
            s = scores + gate_bias
            sv = s.reshape(T, G, E // G)
            top2, _ = lax.top_k(sv, 2)
            group_scores = top2.sum(-1)
            _, gidx = lax.top_k(group_scores, TOPK_G)
            gmask = jnp.zeros((T, G), bool).at[jnp.arange(T)[:, None], gidx].set(True)
            masked = jnp.where(gmask[:, :, None], sv, -jnp.inf).reshape(T, E)
            _, idx = lax.top_k(masked, TOPK)
            w = jnp.take_along_axis(scores, idx, axis=1)
            w = w / (w.sum(-1, keepdims=True) + 1e-06) * ROUTE_SCALE
            return (w, idx)
        B, S, D = x.shape
        x2 = x.reshape(-1, D)
        T = x2.shape[0]
        weights, indices = _gate(x2, gate_weight, gate_bias)
        cw = jnp.zeros((T, E), x.dtype).at[jnp.arange(T)[:, None], indices].add(weights)
        h1 = jnp.einsum('td,eid->tei', x2, w1)
        h3 = jnp.einsum('td,eid->tei', x2, w3)
        h = jax.nn.silu(h1) * h3
        y = jnp.einsum('tei,edi,te->td', h, w2, cw)
        z = jax.nn.silu(x2 @ sw1.T) * (x2 @ sw3.T) @ sw2.T
        return (y + z).reshape(B, S, D)
    h = _L0_tok_ref(x, L0_tok_W_lin, L0_tok_b_lin, L0_tok_cls_token)
    h = h + _L0_attn_ref(_layernorm(h, axis=-1), L0_attn_qkv_weight, L0_attn_proj_weight)
    h = h + _L0_ffn_ref(_layernorm(h, axis=-1), L0_ffn_gate_weight, L0_ffn_gate_bias, L0_ffn_w1, L0_ffn_w2, L0_ffn_w3, L0_ffn_sw1, L0_ffn_sw2, L0_ffn_sw3)
    return h

_drawn_inputs = setup_inputs


def setup_inputs(seed=0):
    import zlib

    import numpy as np

    out = dict(_drawn_inputs(seed))
    spreads = {'L0_tok_cls_token': (1.0, 0.2), 'L0_ffn_gate_bias': (0.0, 0.1)}
    factors = {}
    for name, (base, spread) in spreads.items():
        noise = np.random.default_rng([zlib.crc32(name.encode()), seed]).standard_normal(out[name].shape)
        drawn = base * np.exp(spread * noise) if base else spread * noise
        out[name] = jnp.asarray(drawn.astype(out[name].dtype))
    for name, factor in factors.items():
        out[name] = (out[name] * factor).astype(out[name].dtype)
    return out
```

```python
from contextlib import ExitStack

import concourse.bass as bass
from concourse import mybir

F32 = mybir.dt.float32
F16 = mybir.dt.float16
ACT = mybir.ActivationFunctionType
ALU = mybir.AluOpType
AX = mybir.AxisListType

IMAGES = 64
CHANNELS, SIDE, GRID = 3, 224, 14
PS = SIDE // GRID
PATCHES = GRID * GRID
TOKENS = PATCHES + 1
PCHUNKS = CHANNELS * PS * PS // 128
TR = 99
SLOTS = 2 * TR
KEYS = (TR - 1, TR)
C = 192
KC = C // 2
HEADS, D = 12, 16
PAIRS = HEADS // 2
GROUPS = 2 * PAIRS
QB = 64
TRIO = 3
TRIOS = HEADS // TRIO
TB = TRIO * (2 * D + 1)
EXPERTS, INTER = 8, 128
NE = EXPERTS + 1
EGROUPS = 4
TOTAL = IMAGES * TOKENS
LANES = 4
GT = 128 * LANES
FULL = TOTAL // GT
REST = (TOTAL - FULL * GT) // LANES

SX = 64.0
SW = 256.0
SS = SX * SW
SV = 16.0
SQ = 16.0
SA = 64.0
EPS = 1e-5
UNROLL = 4


def reached(value):
    return not isinstance(value, int) or value > 0


def settle(eng, settled):
    eng.sem_inc(settled, 1)


class Index:

    def __init__(self, i, c, unroll=UNROLL, limit=IMAGES):
        self.i, self.c, self.unroll, self.limit = i, c, unroll, limit

    def back(self, d):
        return Index(self.i, self.c - d, self.unroll, self.limit)

    @property
    def known(self):
        return isinstance(self.i, int)

    def active(self):
        return not self.known or 0 <= self.unroll * self.i + self.c < self.limit

    def times(self, per, plus=0):
        return self.i * (self.unroll * per) + (self.c * per + plus)

    def halves(self, per, plus=0):
        return self.i * (self.unroll // 2 * per) + (self.c // 2 * per + plus)

    def mod(self, m):
        return self.c % m


def vit_layer(nc, xp, w_lin, bias_cls, w_qkv, w_proj, w_gate, gate_bias, w13, w2,
              ident, before4, before8, out):
    hidden_dram = nc.dram_tensor("hidden_dram", [IMAGES, TOKENS, C], F32).ap()
    with ExitStack() as ctx:
        def sb(name, shape, dt=F32):
            return ctx.enter_context(nc.sbuf_tensor(name, shape, dt))

        def sem(name):
            return ctx.enter_context(nc.semaphore(name))

        with ExitStack():
            def stage(name, shape):
                return sb(name, shape)

            def split_pair(name, shape):
                return sb(name + "_hi", shape, F16), sb(name + "_lo", shape, F16)

            lin_hi, lin_lo = split_pair("lin", [128, PCHUNKS, C])
            qkv_hi, qkv_lo = split_pair("qkv", [KC, 2, 3 * C])
            proj_hi, proj_lo = split_pair("proj", [KC, 2, C])
            gate_hi, gate_lo = split_pair("gate", [KC, 2, EXPERTS])
            w13_hi, w13_lo = split_pair("w13", [KC, 2, NE, 2, INTER])
            w2_hi, w2_lo = split_pair("w2", [INTER, NE, C])
            id32 = sb("id32", [128, 128])
            id16 = sb("id16", [128, 128], F16)
            biascls = sb("biascls", [TR, 2, C])
            gbias = sb("gbias", [128, LANES, EXPERTS])
            bef4 = sb("bef4", [128, EGROUPS, EGROUPS])
            bef8 = sb("bef8", [128, EXPERTS, EXPERTS])
            eps = sb("eps", [128, 1])
            minus_half = sb("minus_half", [128, LANES])
            eps_qk = sb("eps_qk", [128, 1])

            lin_f = stage("lin_f", [128, PCHUNKS, C])
            qkv_f = stage("qkv_f", [KC, 2, 3 * C])
            proj_f = stage("proj_f", [KC, 2, C])
            gate_f = stage("gate_f", [KC, 2, EXPERTS])
            w13_f = stage("w13_f", [KC, 2, NE, 2, INTER])
            w2_f = stage("w2_f", [INTER, NE, C])
            qk_mean = stage("qk_mean", [KC, 2, 2 * HEADS])
            weights = [(lin_f, lin_hi, lin_lo, w_lin), (qkv_f, qkv_hi, qkv_lo, w_qkv),
                       (proj_f, proj_hi, proj_lo, w_proj), (gate_f, gate_hi, gate_lo, w_gate),
                       (w13_f, w13_hi, w13_lo, w13), (w2_f, w2_hi, w2_lo, w2)]
            others = [(id32, ident), (biascls, bias_cls), (gbias, gate_bias), (bef4, before4), (bef8, before8)]

            xin = [sb(f"xin{p}", [128, PCHUNKS, SLOTS]) for p in range(2)]
            x_hi = [sb(f"x_hi{p}", [128, PCHUNKS, SLOTS], F16) for p in range(2)]
            x_lo = [sb(f"x_lo{p}", [128, PCHUNKS, SLOTS], F16) for p in range(2)]
            h = [sb(f"h{p}", [TR, 2, C]) for p in range(4)]
            stats = sb("stats", [TR, 2, 6])
            meanvar = sb("meanvar", [TR, 2, 2])
            h_rstd = sb("h_rstd", [TR, 2])
            h_lnvar = sb("h_lnvar", [TR, 2])
            xnorm = sb("xnorm", [TR, 2, C])
            xT_hi = sb("xT_hi", [KC, 2, SLOTS], F16)
            xT_lo = sb("xT_lo", [KC, 2, SLOTS], F16)
            qk_sq = sb("qk_sq", [TR, 2 * HEADS, D])
            qk_var = sb("qk_var", [TR, 2 * HEADS])
            qk_lnvar = sb("qk_lnvar", [TR, 2 * HEADS])
            qk_rstd = sb("qk_rstd", [TR, 2 * HEADS])
            qk_norm = [sb(f"qk_norm{t}", [TR, 2 * HEADS, D]) for t in range(2)]
            qk_split = [sb(f"qk_split{t}", [TR, 2 * HEADS, QB], F16) for t in range(2)]
            qT = [sb(f"qT{p}", [128, PAIRS, SLOTS], F16) for p in range(2)]
            kT = [[sb(f"kT{p}{hh}", [128, PAIRS, SLOTS], F16) for hh in range(2)] for p in range(2)]
            v_f = sb("v_f", [TR, 2, HEADS, D])
            v = [sb(f"v{p}", [TR, 2, HEADS, TB], F16) for p in range(2)]
            prob = [sb(f"prob{r}", [TR, 2, SLOTS]) for r in range(4)]
            prob_hi = [sb(f"prob_hi{r}", [TR, 2, SLOTS], F16) for r in range(4)]
            prob_lo = [sb(f"prob_lo{r}", [TR, 2, SLOTS], F16) for r in range(4)]
            oT = sb("oT", [TB, TRIOS, SLOTS])
            o_sum = sb("o_sum", [TR, 2, HEADS, D])
            o_rden = sb("o_rden", [TR, 2, HEADS])
            o_norm = sb("o_norm", [TR, 2, C])
            onT_hi = sb("onT_hi", [KC, 2, SLOTS], F16)
            onT_lo = sb("onT_lo", [KC, 2, SLOTS], F16)
            h2 = [sb(f"h2{p}", [TR, 2, C]) for p in range(2)]

            w_loaded = [sem(f"w_loaded{n}") for n in range(len(weights))]
            consts_loaded = sem("consts_loaded")
            w_centred = sem("w_centred")
            w_hi_done = sem("w_hi_done")
            w_lo_done = sem("w_lo_done")
            consts_set = sem("consts_set")
            v_zeroed = sem("v_zeroed")

            with nc.Block() as block:
                @block.sync
                def _(sp):
                    for n, (f, _, _, dram) in enumerate(weights):
                        sp.dma_start(f[:], dram).then_inc(w_loaded[n], 16)
                    for tile, dram in others:
                        sp.dma_start(tile[:], dram).then_inc(consts_loaded, 16)
                    sp.wait_ge(consts_loaded, 16 * len(others))

                @block.scalar
                def _(act):
                    for n, (f, hi, _, _) in enumerate(weights):
                        act.wait_ge(w_loaded[n], 16)
                        if n == 1:
                            act.wait_ge(w_centred, 3)
                        act.activation(hi[:], f[:], ACT.Copy, scale=SW).then_inc(w_hi_done, 1)
                    act.wait_ge(consts_loaded, 16 * len(others))
                    act.activation(id16[:], id32[:], ACT.Copy).then_inc(consts_set, 1)

                @block.vector
                def _(dve):
                    dve.wait_ge(w_loaded[1], 16)
                    for k in range(2):
                        qk = qkv_f[:, k, 0:2 * C].rearrange("p (h d) -> p h d", d=D)
                        dve.tensor_reduce(qk_mean[:, k, :], qk, AX.X, ALU.add).then_inc(w_centred, 1)
                    dve.wait_ge(w_centred, 2)
                    dve.tensor_scalar(qk_mean[:], qk_mean[:], 1.0 / D, None, ALU.mult).then_inc(w_lo_done, 1)
                    dve.wait_ge(w_lo_done, 1)
                    for k in range(2):
                        qk = qkv_f[:, k, 0:2 * C].rearrange("p (h d) -> p h d", d=D)
                        mean = qk_mean[:, k, :].unsqueeze(2).broadcast_to([KC, 2 * HEADS, D])
                        last = dve.tensor_tensor(qk, qk, mean, ALU.subtract)
                    last.then_inc(w_centred, 1)
                    for n, (f, hi, lo, _) in enumerate(weights):
                        dve.wait_ge(w_hi_done, n + 1)
                        dve.scalar_tensor_tensor(out=lo[:], in0=f[:], scalar=SW, in1=hi[:],
                                                 op0=ALU.mult, op1=ALU.subtract).then_inc(w_lo_done, 1)

                @block.gpsimd
                def _(pool):
                    pool.memset(eps[:], EPS)
                    pool.memset(minus_half[:], -0.5)
                    pool.memset(eps_qk[:], (SS / SQ) ** 2 * EPS)
                    for t in range(2):
                        pool.memset(qk_split[t][:], 0.0)
                    for p in range(2):
                        for hh in range(2):
                            pool.memset(kT[p][hh][:], 0.0)
                        pool.memset(v[p][:], 0.0).then_inc(v_zeroed, 1)
                    pool.wait_ge(v_zeroed, 2)
                    for p in range(2):
                        for i in range(TRIO):
                            of_head = v[p][:].rearrange("p t (g i) e -> p (t g) i e", i=TRIO)[:, :, i, :]
                            at = TRIO * 2 * D + i
                            last = pool.memset(of_head[:, :, at:at + 1], SV)
                    last.then_inc(consts_set, 1)
                    pool.wait_ge(consts_set, 2)

        phase_a(nc, xp, hidden_dram, sem, locals())
        phase_b(nc, hidden_dram, out, sem, sb, locals())


def phase_a(nc, xp, hidden_dram, sem, bufs):
    (lin_hi, lin_lo, qkv_hi, qkv_lo, proj_hi, proj_lo, id32, id16, biascls, eps, eps_qk, xin, x_hi, x_lo,
     h, stats, meanvar, h_rstd, h_lnvar, xnorm, xT_hi, xT_lo, qk_sq, qk_var, qk_lnvar, qk_rstd,
     qk_norm, qk_split, qT, kT, v_f, v, prob, prob_hi, prob_lo, oT, o_sum, o_rden, o_norm, onT_hi, onT_lo, h2) = (
        bufs[n] for n in (
            "lin_hi lin_lo qkv_hi qkv_lo proj_hi proj_lo id32 id16 biascls eps eps_qk xin x_hi x_lo "
            "h stats meanvar h_rstd h_lnvar xnorm xT_hi xT_lo qk_sq qk_var qk_lnvar qk_rstd "
            "qk_norm qk_split qT kT v_f v prob prob_hi prob_lo oT o_sum o_rden o_norm onT_hi onT_lo h2").split())
    with ExitStack() as ctx:
        def ps(name, shape, dt=F32):
            return ctx.enter_context(nc.psum_tensor(name, shape, dt))

        ps_hid = ps("ps_hid", [128, 512])
        ps_tr = ps("ps_tr", [128, 512])
        ps_qk = ps("ps_qk", [128, 512])
        ps_qkT = ps("ps_qkT", [128, 1024], F16)
        ps_sc = [ps(f"ps_sc{b}", [128, 512]) for b in range(2)]
        ps_o = [ps(f"ps_o{t}", [128, 512]) for t in range(2)]
        hid = ps_hid[0:TR, 0:2 * C].rearrange("p (t c) -> p t c", t=2)
        tok = ps_tr[0:TR, 0:2 * C].rearrange("p (t c) -> p t c", t=2)
        feat = ps_tr[0:KC, 0:2 * SLOTS].rearrange("p (k s) -> p k s", k=2)
        qk_ps = ps_qk[0:TR, 0:2 * C].rearrange("p (h d) -> p h d", d=D)
        TRP = TR + 1
        qkT_ps = ps_qkT[:, 0:PAIRS * TRP].rearrange("p (b s) -> p b s", s=TRP)
        sc = [b[:, 0:2 * SLOTS].rearrange("p (h s) -> p h s", h=2) for b in ps_sc]
        oT_ps = [b[0:TB, 0:2 * SLOTS].rearrange("p (g s) -> p g s", g=2) for b in ps_o]

        x_in = [sem(f"x_in{p}") for p in range(2)]
        h2_out = [sem(f"h2_out{p}") for p in range(2)]
        hid_done, xT_done, qk_done, v_done = sem("hid_done"), sem("xT_done"), sem("qk_done"), sem("v_done")
        qkT_done, sc_done, av_done = sem("qkT_done"), sem("sc_done"), sem("av_done")
        otok_done, onT_done, proj_done = sem("otok_done"), sem("onT_done"), sem("proj_done")
        xhi_done, xThi_done, sq_done, exp_done = sem("xhi_done"), sem("xThi_done"), sem("sq_done"), sem("exp_done")
        qkT_out, vf_done, oT_out, onThi_done = sem("qkT_out"), sem("vf_done"), sem("oT_out"), sem("onThi_done")
        xlo_done, h_done, stats_done, mv_done = sem("xlo_done"), sem("h_done"), sem("stats_done"), sem("mv_done")
        xnorm_done, xTlo_done, qkvar_done, qknorm_done = (
            sem("xnorm_done"), sem("xTlo_done"), sem("qkvar_done"), sem("qknorm_done"))
        phi_done, plo_done = sem("phi_done"), sem("plo_done")
        o_read, rden_done, onorm_done, onTlo_done, h2_done = (
            sem("o_read"), sem("rden_done"), sem("onorm_done"), sem("onTlo_done"), sem("h2_done"))
        hln_done, hrstd_done, qkln_done, qkrstd_done, qkhi_done = (
            sem("hln_done"), sem("hrstd_done"), sem("qkln_done"), sem("qkrstd_done"), sem("qkhi_done"))
        qksplit_done = sem("qksplit_done")
        vhi_done, vsplit_done = sem("vhi_done"), sem("vsplit_done")

        def run(fori, step):
            first = 2
            for k in range(first * UNROLL):
                step(Index(0, k))
            with fori(first, IMAGES // UNROLL) as i:
                for c in range(UNROLL):
                    step(Index(i, c))
            for k in range(IMAGES, IMAGES + 4):
                step(Index(0, k))

        block = ctx.enter_context(nc.Block())

        @block.sync
        def _(sp):
            def load(n):
                p = n.mod(2)
                if reached(n.times(1, -1)):
                    sp.wait_ge(xhi_done, n.times(1, -1))
                if reached(n.times(1, -1)):
                    sp.wait_ge(xlo_done, n.times(1, -1))
                sp.dma_start(xin[p][:], xp[n.times(1)]).then_inc(x_in[p], 16)

            def store(n):
                p = n.mod(2)
                sp.wait_ge(h2_done, n.times(1, 1))
                image = hidden_dram[n.times(1)]
                sp.dma_start(image[1:TOKENS].rearrange("(t p) c -> p t c", t=2),
                             h2[p][0:TR - 1, :, :]).then_inc(h2_out[p], 16)
                sp.dma_start(image[0:1], h2[p][TR - 1:TR, 1, :]).then_inc(h2_out[p], 16)

            def step(k):
                if k.active():
                    load(k)
                if k.back(5).active():
                    store(k.back(5))

            run(sp.Fori, step)
            store(Index(0, IMAGES - 1))
            for p in range(2):
                sp.wait_ge(h2_out[p], 32 * (IMAGES // 2))

        @block.tensor
        def _(pe):
            def products(outs, lhs, rhs, chunks):
                (lhs_hi, lhs_lo), (rhs_hi, rhs_lo) = lhs, rhs
                for k in range(chunks):
                    pe.matmul(outs, lhs_hi(k), rhs_hi(k), start=(k == 0), stop=False)
                    pe.matmul(outs, lhs_hi(k), rhs_lo(k), start=False, stop=False)
                    last = pe.matmul(outs, lhs_lo(k), rhs_hi(k), start=False, stop=(k == chunks - 1))
                return last

            def embed(n, t):
                p, s = n.mod(2), slice(t * TR, (t + 1) * TR)
                if t == 0:
                    pe.wait_ge(xhi_done, n.times(1, 1))
                    pe.wait_ge(xlo_done, n.times(1, 1))
                    if reached(n.times(1, -1)):
                        pe.wait_ge(vf_done, n.times(1, -1))
                last = products(hid[:, t, :],
                                (lambda k: x_hi[p][:, k, s], lambda k: x_lo[p][:, k, s]),
                                (lambda k: lin_hi[:, k, :], lambda k: lin_lo[:, k, :]), PCHUNKS)
                if t == 1:
                    last.then_inc(hid_done, 1)

            def transpose_tokens(src, done):
                for t in range(2):
                    for k in range(2):
                        last = pe.transpose(feat[:, k, t * TR:(t + 1) * TR], src[:, t, k * KC:(k + 1) * KC],
                                            id32[0:TR, 0:TR])
                last.then_inc(done, 1)

            def from_xT(outs, t, cols):
                s = slice(t * TR, (t + 1) * TR)
                return products(outs, (lambda k: xT_hi[:, k, s], lambda k: xT_lo[:, k, s]),
                                (lambda k: qkv_hi[:, k, cols], lambda k: qkv_lo[:, k, cols]), 2)

            def qk(n, t):
                if t == 0:
                    pe.wait_ge(xThi_done, n.times(1, 1))
                    pe.wait_ge(xTlo_done, n.times(1, 1))
                if reached(n.times(2, t)):
                    pe.wait_ge(qknorm_done, n.times(2, t))
                from_xT(ps_qk[0:TR, 0:2 * C], t, slice(0, 2 * C)).then_inc(qk_done, 1)

            def values(n, embedded):
                if embedded.active():
                    pe.wait_ge(h_done, embedded.times(1, 1))
                for t in range(2):
                    last = from_xT(hid[:, t, :], t, slice(2 * C, 3 * C))
                last.then_inc(v_done, 1)

            def transpose_qk(n, t, w):
                if w == 0:
                    pe.wait_ge(qksplit_done, n.times(2, t + 1))
                if reached(n.times(4, 2 * t + w)):
                    pe.wait_ge(qkT_out, n.times(4, 2 * t + w))
                part = qk_split[t][:, w * HEADS:(w + 1) * HEADS, :].rearrange("p (b h) e -> p b (h e)", h=2)
                for b in range(PAIRS):
                    last = pe.transpose(qkT_ps[:, b, 0:TR], part[:, b, :], id16[0:TR, 0:TR])
                last.then_inc(qkT_done, 1)

            def scores(n, j):
                p, pair, m = n.mod(2), j // 2, j % 2
                if j == 0:
                    pe.wait_ge(qkT_out, n.times(4, 4))
                if reached(n.times(GROUPS, j - 1)):
                    pe.wait_ge(exp_done, n.times(GROUPS, j - 1))
                for hh in range(2):
                    last = pe.matmul(sc[j % 2][0:KEYS[m], hh, :], kT[p][hh][:, pair, m * TR:m * TR + KEYS[m]],
                                     qT[p][:, pair, :], start=True, stop=True)
                last.then_inc(sc_done, 1)

            def attend(n, pair):
                p = n.mod(2)
                if pair == 0:
                    pe.wait_ge(vsplit_done, n.times(1, 1))
                for hh in range(2):
                    trio, place = divmod(2 * pair + hh, TRIO)
                    if place == 0 and trio % 2 == 0:
                        if reached(n.times(2, trio // 2 - 1)):
                            pe.wait_ge(oT_out, n.times(2, trio // 2 - 1))
                    if hh == 0:
                        pe.wait_ge(plo_done, n.times(GROUPS, 2 * pair + 2))
                    dst = oT_ps[trio // 2][:, trio % 2, :]
                    for m in range(2):
                        r, rows = (2 * pair + m) % 4, slice(0, KEYS[m])
                        own = v[p][rows, m, 2 * pair + hh, :]
                        pe.matmul(dst, own, prob_hi[r][rows, hh, :], start=(place == 0 and m == 0), stop=False)
                        last = pe.matmul(dst, own, prob_lo[r][rows, hh, :], start=False,
                                         stop=(place == TRIO - 1 and m == 1))
                last.then_inc(av_done, 1)

            def o_by_token(n, t):
                if t == 0:
                    pe.wait_ge(oT_out, n.times(2, 2))
                else:
                    pe.wait_ge(o_read, n.times(2, 1))
                for g in range(TRIOS):
                    last = pe.transpose(ps_tr[0:TR, g * TB:(g + 1) * TB], oT[:, g, t * TR:(t + 1) * TR],
                                        id32[0:TB, 0:TB])
                last.then_inc(otok_done, 1)

            def project(n):
                pe.wait_ge(onThi_done, n.times(1, 1))
                pe.wait_ge(onTlo_done, n.times(1, 1))
                for t in range(2):
                    s = slice(t * TR, (t + 1) * TR)
                    last = products(tok[:, t, :], (lambda k: onT_hi[:, k, s], lambda k: onT_lo[:, k, s]),
                                    (lambda k: proj_hi[:, k, :], lambda k: proj_lo[:, k, :]), 2)
                last.then_inc(proj_done, 1)

            def step(k):
                n1, n2, n3, n4 = (k.back(d) for d in (1, 2, 3, 4))
                for slot in range(PAIRS):
                    if n3.active():
                        scores(n3, 2 * slot)
                        scores(n3, 2 * slot + 1)
                    if n2.active():
                        if slot < 2:
                            qk(n2, slot)
                        else:
                            transpose_qk(n2, (slot - 2) // 2, slot % 2)
                    if slot == 0 and n4.active():
                        attend(n4, PAIRS - 1)
                    if slot > 0 and n3.active():
                        attend(n3, slot - 1)
                    if slot == 1 and n1.active():
                        embed(n1, 0)
                    if slot == 2 and n1.active():
                        embed(n1, 1)
                    if slot == 1 and n4.active():
                        if n2.active():
                            pe.wait_ge(xThi_done, n2.times(1, 1))
                            pe.wait_ge(xTlo_done, n2.times(1, 1))
                        o_by_token(n4, 0)
                    if slot == 2 and n4.active():
                        o_by_token(n4, 1)
                    if slot == 3 and n4.active():
                        pe.wait_ge(onorm_done, n4.times(1, 1))
                        transpose_tokens(o_norm, onT_done)
                    if slot == 4 and n2.active():
                        values(n2, n1)
                    if slot == 4 and n4.active():
                        project(n4)
                    if slot == 5 and n1.active():
                        if n4.active():
                            pe.wait_ge(h2_done, n4.times(1, 1))
                        elif n2.active():
                            pe.wait_ge(xThi_done, n2.times(1, 1))
                            pe.wait_ge(xTlo_done, n2.times(1, 1))
                        pe.wait_ge(xnorm_done, n1.times(1, 1))
                        transpose_tokens(xnorm, xT_done)

            run(pe.Fori, step)

        @block.scalar
        def _(act):
            act.preload_act_table_set("natural_log_exp_and_others")

            def split_x(n):
                p = n.mod(2)
                act.wait_ge(x_in[p], n.halves(16, 16))
                if reached(n.times(1, -1)):
                    act.wait_ge(hid_done, n.times(1, -1))
                act.activation(x_hi[p][:], xin[p][:], ACT.Copy, scale=SX).then_inc(xhi_done, 1)

            def xT_out(n):
                act.wait_ge(xT_done, n.times(1, 1))
                if reached(n.times(1)):
                    act.wait_ge(v_done, n.times(1))
                act.activation(xT_hi[:], feat, ACT.Copy, scale=SX).then_inc(xThi_done, 1)

            def square(n, t):
                act.wait_ge(qk_done, n.times(2, t + 1))
                if reached(n.times(2, t)):
                    act.wait_ge(qkvar_done, n.times(2, t))
                act.activation(qk_sq[:], qk_ps, ACT.Square, scale=1.0 / SS).then_inc(sq_done, 1)

            def h_rstds(n):
                act.wait_ge(mv_done, n.times(2, 2))
                act.activation(h_lnvar[:], meanvar[:, :, 1], ACT.Ln, bias=eps[0:TR]).then_inc(hln_done, 1)
                act.wait_ge(hln_done, n.times(1, 1))
                act.activation(h_rstd[:], h_lnvar[:], ACT.Exp, scale=-0.5).then_inc(hrstd_done, 1)

            def qk_rstds(n, t):
                act.wait_ge(qkvar_done, n.times(2, t + 1))
                act.activation(qk_lnvar[:], qk_var[:], ACT.Ln, bias=eps_qk[0:TR],
                               scale=(SS / SQ) ** 2 / D).then_inc(qkln_done, 1)
                act.wait_ge(qkln_done, n.times(2, t + 1))
                act.activation(qk_rstd[:], qk_lnvar[:], ACT.Exp, scale=-0.5).then_inc(qkrstd_done, 1)

            def qk_first(n, t):
                act.wait_ge(qknorm_done, n.times(2, t + 1))
                if reached(n.times(4, 2 * t - 2)):
                    act.wait_ge(qkT_done, n.times(4, 2 * t - 2))
                f, s = qk_norm[t], qk_split[t]
                q, k = slice(0, HEADS), slice(HEADS, 2 * HEADS)
                act.activation(s[:, :, 0:D], f[:], ACT.Copy)
                act.activation(s[:, q, D:2 * D], f[:, q, :], ACT.Copy)
                act.activation(s[:, k, 2 * D:3 * D], f[:, k, :], ACT.Copy).then_inc(qkhi_done, 1)

            def qkT_copy(n, t, w):
                act.wait_ge(qkT_done, n.times(4, 2 * t + w + 1))
                if t == 0:
                    if reached(n.times(GROUPS, -GROUPS)):
                        act.wait_ge(sc_done, n.times(GROUPS, -GROUPS))
                cols = slice(t * TR, (t + 1) * TR)
                if w == 0:
                    act.activation(qT[n.mod(2)][:, :, cols], qkT_ps[:, :, 0:TR], ACT.Copy).then_inc(qkT_out, 1)
                else:
                    for hh in range(2):
                        rows = slice(QB * hh, QB * hh + QB)
                        last = act.activation(kT[n.mod(2)][hh][rows, :, cols], qkT_ps[rows, :, 0:TR], ACT.Copy)
                    last.then_inc(qkT_out, 1)

            def v_copy(n):
                act.wait_ge(v_done, n.times(1, 1))
                if reached(n.times(1)):
                    act.wait_ge(vsplit_done, n.times(1))
                act.activation(v_f[:].rearrange("p t h d -> p (t h d)"), ps_hid[0:TR, 0:2 * C], ACT.Copy,
                               scale=SV / SS).then_inc(vf_done, 1)

            def oT_copy(n, b):
                if reached(n.times(PAIRS, 3 * b + 3)):
                    act.wait_ge(av_done, n.times(PAIRS, 3 * b + 3))
                if reached(n.times(2)):
                    act.wait_ge(otok_done, n.times(2))
                act.activation(oT[:, 2 * b:2 * b + 2, :], oT_ps[b], ACT.Copy).then_inc(oT_out, 1)

            def exponent(n, j):
                rows = slice(0, KEYS[j % 2])
                act.wait_ge(sc_done, n.times(GROUPS, j + 1))
                if reached(n.times(GROUPS, j - 3)):
                    act.wait_ge(plo_done, n.times(GROUPS, j - 3))
                act.activation(prob[j % 4][rows], sc[j % 2][rows], ACT.Exp,
                               scale=D ** -0.5 / (SQ * SQ)).then_inc(exp_done, 1)

            def onT_out(n):
                act.wait_ge(onT_done, n.times(1, 1))
                if reached(n.times(1)):
                    act.wait_ge(proj_done, n.times(1))
                act.activation(onT_hi[:], feat, ACT.Copy, scale=SX).then_inc(onThi_done, 1)

            def step(k):
                n1, n2, n3, n4 = (k.back(d) for d in (1, 2, 3, 4))
                for slot in range(PAIRS):
                    if n3.active():
                        exponent(n3, 2 * slot)
                        exponent(n3, 2 * slot + 1)
                    if n2.active():
                        if slot < 2:
                            square(n2, slot)
                            qk_rstds(n2, slot)
                        if slot == 1 or slot == 2:
                            qk_first(n2, slot - 1)
                        if slot > 1:
                            qkT_copy(n2, (slot - 2) // 2, slot % 2)
                    if slot == 0 and n4.active():
                        oT_copy(n4, 1)
                    if slot == 4 and n3.active():
                        oT_copy(n3, 0)
                    if slot == 3 and n4.active():
                        onT_out(n4)
                    if slot == 4 and n1.active():
                        h_rstds(n1)
                    if slot == 4 and n2.active():
                        v_copy(n2)
                    if slot == 4 and k.active():
                        split_x(k)
                    if slot == 5 and n1.active():
                        xT_out(n1)

            run(act.Fori, step)

        @block.vector
        def _(dve):
            settled = sem("dve_settled_a")

            def split_x(n):
                p = n.mod(2)
                dve.wait_ge(xhi_done, n.times(1, 1))
                dve.scalar_tensor_tensor(out=x_lo[p][:], in0=xin[p][:], scalar=SX, in1=x_hi[p][:],
                                         op0=ALU.mult, op1=ALU.subtract).then_inc(xlo_done, 1)

            def hidden(n):
                q = n.mod(4)
                dve.wait_ge(hid_done, n.times(1, 1))
                if reached(n.times(1, -3)):
                    dve.wait_ge(h2_done, n.times(1, -3))
                dve.scalar_tensor_tensor(out=h[q][:], in0=hid, scalar=1.0 / SS, in1=biascls[:],
                                         op0=ALU.mult, op1=ALU.add).then_inc(h_done, 1)
                dve.wait_ge(h_done, n.times(1, 1))
                for t in range(2):
                    dve.bn_stats(stats[:, t, :], h[q][:, t, :]).then_inc(stats_done, 1)
                dve.wait_ge(stats_done, n.times(2, 2))
                settle(dve, settled)
                for t in range(2):
                    dve.bn_aggr(meanvar[:, t, :], stats[:, t, :]).then_inc(mv_done, 1)

            def norm_hidden(n):
                dve.wait_ge(hrstd_done, n.times(1, 1))
                if reached(n.times(1)):
                    dve.wait_ge(xT_done, n.times(1))
                for t in range(2):
                    last = dve.tensor_scalar(xnorm[:, t, :], h[n.mod(4)][:, t, :], meanvar[:, t, 0:1],
                                             h_rstd[:, t:t + 1], ALU.subtract, ALU.mult)
                last.then_inc(xnorm_done, 1)

            def xT_out(n):
                dve.wait_ge(xThi_done, n.times(1, 1))
                dve.scalar_tensor_tensor(out=xT_lo[:], in0=feat, scalar=SX, in1=xT_hi[:],
                                         op0=ALU.mult, op1=ALU.subtract).then_inc(xTlo_done, 1)

            def qk_variance(n, t):
                dve.wait_ge(sq_done, n.times(2, t + 1))
                dve.tensor_reduce(qk_var[:], qk_sq[:], AX.X, ALU.add).then_inc(qkvar_done, 1)

            def qk_normalise(n, t):
                dve.wait_ge(qkrstd_done, n.times(2, t + 1))
                if reached(n.times(2, t - 1)):
                    dve.wait_ge(qksplit_done, n.times(2, t - 1))
                dve.tensor_tensor(qk_norm[t][:], qk_ps, qk_rstd[:].unsqueeze(2).broadcast_to([TR, 2 * HEADS, D]),
                                  ALU.mult).then_inc(qknorm_done, 1)

            def prob_first(n, j):
                rows, r = slice(0, KEYS[j % 2]), j % 4
                dve.wait_ge(exp_done, n.times(GROUPS, j + 1))
                if reached(n.times(PAIRS, j // 2 - 1)):
                    dve.wait_ge(av_done, n.times(PAIRS, j // 2 - 1))
                dve.tensor_copy(prob_hi[r][rows], prob[r][rows]).then_inc(phi_done, 1)

            def prob_rest(n, j):
                rows, r = slice(0, KEYS[j % 2]), j % 4
                dve.wait_ge(phi_done, n.times(GROUPS, j + 1))
                dve.tensor_tensor(prob_lo[r][rows], prob[r][rows], prob_hi[r][rows],
                                  ALU.subtract).then_inc(plo_done, 1)

            def o_out(n, t):
                dve.wait_ge(otok_done, n.times(2, t + 1))
                trios = ps_tr[0:TR, 0:TRIOS * TB].rearrange("p (g e) -> p g e", e=TB)
                dve.reciprocal(o_rden[:, t, :].rearrange("p (g i) -> p g i", i=TRIO),
                               trios[:, :, TRIO * 2 * D:TB]).then_inc(rden_done, 1)
                parts = trios[:, :, 0:TRIO * 2 * D].rearrange("p g (i two d) -> p g i d two", two=2, d=D)
                dve.tensor_reduce(o_sum[:, t, :, :].rearrange("p (g i) d -> p g i d", i=TRIO), parts,
                                  AX.X, ALU.add).then_inc(o_read, 1)

            def o_normalise(n):
                dve.wait_ge(rden_done, n.times(2, 2))
                dve.wait_ge(o_read, n.times(2, 2))
                if reached(n.times(1)):
                    dve.wait_ge(onT_done, n.times(1))
                dve.tensor_tensor(o_norm[:].rearrange("p t (h d) -> p (t h) d", d=D),
                                  o_sum[:].rearrange("p t h d -> p (t h) d"),
                                  o_rden[:].rearrange("p t h -> p (t h)").unsqueeze(2)
                                  .broadcast_to([TR, 2 * HEADS, D]), ALU.mult).then_inc(onorm_done, 1)

            def onT_out(n):
                dve.wait_ge(onThi_done, n.times(1, 1))
                dve.scalar_tensor_tensor(out=onT_lo[:], in0=feat, scalar=SX, in1=onT_hi[:],
                                         op0=ALU.mult, op1=ALU.subtract).then_inc(onTlo_done, 1)

            def residual(n):
                p = n.mod(2)
                dve.wait_ge(proj_done, n.times(1, 1))
                if reached(n.halves(32)):
                    dve.wait_ge(h2_out[p], n.halves(32))
                dve.scalar_tensor_tensor(out=h2[p][:], in0=tok, scalar=1.0 / SS, in1=h[n.mod(4)][:],
                                         op0=ALU.mult, op1=ALU.add).then_inc(h2_done, 1)

            def step(k):
                n1, n2, n3, n4 = (k.back(d) for d in (1, 2, 3, 4))
                for slot in range(PAIRS):
                    if n2.active() and slot < 2:
                        qk_variance(n2, slot)
                    for part in (prob_first, prob_rest):
                        for j in range(2):
                            if slot == 0 and n4.active():
                                part(n4, GROUPS - 2 + j)
                            if slot > 0 and n3.active():
                                part(n3, 2 * slot - 2 + j)
                    if n2.active():
                        if slot < 2:
                            qk_normalise(n2, slot)
                    if n4.active():
                        if slot == 1:
                            o_out(n4, 0)
                        if slot == 2:
                            o_out(n4, 1)
                            o_normalise(n4)
                        if slot == 4:
                            onT_out(n4)
                        if slot == 5:
                            residual(n4)
                    if n1.active():
                        if slot == 3:
                            hidden(n1)
                        if slot == 4:
                            norm_hidden(n1)
                        if slot == 5:
                            xT_out(n1)
                    if k.active() and slot == 5:
                        split_x(k)

            run(dve.Fori, step)

        @block.gpsimd
        def _(pool):
            settled = sem("pool_settled_a")

            def qk_rest(n, t):
                pool.wait_ge(qkhi_done, n.times(2, t + 1))
                f, s = qk_norm[t], qk_split[t]
                q, k = slice(0, HEADS), slice(HEADS, 2 * HEADS)
                pool.tensor_tensor(s[:, q, 2 * D:3 * D], f[:, q, :], s[:, q, 0:D], ALU.subtract)
                pool.tensor_tensor(s[:, k, D:2 * D], f[:, k, :], s[:, k, 0:D],
                                   ALU.subtract).then_inc(qksplit_done, 1)

            def split_v(n):
                p = n.mod(2)
                pool.wait_ge(vf_done, n.times(1, 1))
                if reached(n.times(PAIRS, -PAIRS)):
                    pool.wait_ge(av_done, n.times(PAIRS, -PAIRS))
                settle(pool, settled)
                own = [v_at(p, t, 0) for t in range(2)]
                rest = [v_at(p, t, D) for t in range(2)]
                for t in range(2):
                    f = v_f[:, t].rearrange("p (g i) d -> p g i d", i=TRIO)
                    pool.tensor_copy(own[t], f).then_inc(vhi_done, 1)
                pool.wait_ge(vhi_done, n.times(2, 2))
                for t in range(2):
                    f = v_f[:, t].rearrange("p (g i) d -> p g i d", i=TRIO)
                    last = pool.tensor_tensor(rest[t], f, own[t], ALU.subtract)
                last.then_inc(vsplit_done, 1)

            def v_at(p, t, plus):
                tile = v[p][:, t, :, :]
                return bass.AP(tensor=tile.tensor, offset=tile.offset + plus,
                               ap=[[tile.ap[0][0], TR], [TRIO * TB, TRIOS], [TB + 2 * D, TRIO], [1, D]])

            def step(k):
                n2 = k.back(2)
                for slot in range(PAIRS):
                    if n2.active() and slot < 2:
                        qk_rest(n2, slot)
                    if n2.active() and slot == 5:
                        split_v(n2)

            run(pool.Fori, step)


def phase_b(nc, hidden_dram, out, sem, sb, bufs):
    w13_hi, w13_lo, w2_hi, w2_lo, gate_hi, gate_lo, id32, gbias, bef4, bef8, minus_half = (
        bufs[n] for n in "w13_hi w13_lo w2_hi w2_lo gate_hi gate_lo id32 gbias bef4 bef8 minus_half".split())
    with ExitStack() as ctx:
        def ps(name, shape, dt=F32):
            return ctx.enter_context(nc.psum_tensor(name, shape, dt))

        T, E, G = LANES, EXPERTS, EGROUPS
        acc = [sb(f"acc{p}", [128, T, C]) for p in range(2)]
        bstats = sb("bstats", [128, T, 6])
        bmv = sb("bmv", [128, T, 2])
        bvareps = sb("bvareps", [128, T])
        brstd = sb("brstd", [128, T])
        bnorm = sb("bnorm", [128, T, C])
        yT_hi = [sb(f"yT_hi{p}", [KC, 2, GT], F16) for p in range(2)]
        yT_lo = [sb(f"yT_lo{p}", [KC, 2, GT], F16) for p in range(2)]
        act1 = [sb(f"act1{p}", [INTER, GT]) for p in range(2)]
        inner = [sb(f"inner{p}", [INTER, GT]) for p in range(2)]
        in_hi = [sb(f"in_hi{p}", [INTER, GT], F16) for p in range(2)]
        in_lo = [sb(f"in_lo{p}", [INTER, GT], F16) for p in range(2)]
        half = sb("half", [128, T, E])
        score = sb("score", [128, T, E])
        biased = sb("biased", [128, T, E])
        gsum = sb("gsum", [128, T, G])
        cmp4 = sb("cmp4", [128, T, G, G])
        eq4 = sb("eq4", [128, T, G, G])
        rank4 = sb("rank4", [128, T, G])
        chosen4 = sb("chosen4", [128, T, G])
        drop4 = sb("drop4", [128, T, G])
        masked = sb("masked", [128, T, E])
        cmp8 = sb("cmp8", [128, T, E, E])
        eq8 = sb("eq8", [128, T, E, E])
        rank8 = sb("rank8", [128, T, E])
        wsel = sb("wsel", [128, T, E])
        den = sb("den", [128, T])
        rden = sb("rden", [128, T])
        comb = [sb(f"comb{p}", [128, T, E]) for p in range(2)]

        ps_h1 = [ps(f"ps_h1{b}", [128, 512]) for b in range(2)]
        ps_h3 = [ps(f"ps_h3{b}", [128, 512]) for b in range(2)]
        ps_y = [ps(f"ps_y{b}", [128, 512]) for b in range(2)]
        ps_x = [ps(f"ps_x{k}", [128, 512]) for k in range(2)]

        acc_in = [sem(f"acc_in{p}") for p in range(2)]
        acc_out = [sem(f"acc_out{p}") for p in range(2)]
        yT_done, gate_done, inner_done, y_done = sem("yT_done"), sem("gate_done"), sem("inner_done"), sem("y_done")
        yThi_done, tanh_done, silu_done, inhi_done = (
            sem("yThi_done"), sem("tanh_done"), sem("silu_done"), sem("inhi_done"))
        bst_done, bmv_done, bnorm_done, yTlo_done = (
            sem("bst_done"), sem("bmv_done"), sem("bnorm_done"), sem("yTlo_done"))
        route_step, route_done = sem("route_step"), sem("route_done")
        mul_done, inlo_done, acc_done = sem("mul_done"), sem("inlo_done"), sem("acc_done")
        bve_done, brstd_done = sem("bve_done"), sem("brstd_done")

        tokens_in = hidden_dram.rearrange("n t c -> (n t) c")
        tokens_out = out.rearrange("n t c -> (n t) c")
        LAST = FULL
        GROUPS_B = FULL + 1

        def rows_of(g):
            return REST if g.known and g.i * 2 + g.c == LAST else 128

        def full(dram):
            return dram[0:FULL * GT].rearrange("(g p t) c -> g p t c", p=128, t=T)

        def part(dram, g):
            if rows_of(g) == 128:
                return full(dram)[g.times(1)]
            return dram[FULL * GT:TOTAL].rearrange("(p t) c -> p t c", t=T)

        def run(fori, body):
            def at(i, c):
                return Index(i, c, 2, GROUPS_B)
            body(at(0, 0))
            with fori(0, (FULL - 2) // 2) as i:
                for c in (1, 2):
                    body(at(i, c))
            body(at(0, FULL - 1))
            body(at(0, FULL))

        block = ctx.enter_context(nc.Block())

        @block.sync
        def _(sp):
            def load(g):
                p = g.mod(2)
                if reached(g.halves(16)):
                    sp.wait_ge(acc_out[p], g.halves(16))
                sp.dma_start(acc[p][0:rows_of(g)], part(tokens_in, g)).then_inc(acc_in[p], 16)

            def store(g):
                p = g.mod(2)
                sp.wait_ge(acc_done, g.times(2 * NE, 2 * NE))
                sp.dma_start(part(tokens_out, g), acc[p][0:rows_of(g)]).then_inc(acc_out[p], 16)

            load(Index(0, 0, 2, GROUPS_B))

            def body(g):
                if g.back(-1).active():
                    load(g.back(-1))
                store(g)
            run(sp.Fori, body)
            sp.wait_ge(acc_out[0], 16 * (FULL // 2 + 1))
            sp.wait_ge(acc_out[1], 16 * (FULL // 2))

        @block.tensor
        def _(pe):
            def transposes(g):
                R = rows_of(g)
                pe.wait_ge(bnorm_done, g.times(1, 1))
                if reached(g.times(1)):
                    pe.wait_ge(tanh_done, g.times(1))
                for k in range(2):
                    for t in range(T):
                        last = pe.transpose(ps_x[k][0:KC, t * R:(t + 1) * R], bnorm[0:R, t, k * KC:(k + 1) * KC],
                                            id32[0:R, 0:R])
                last.then_inc(yT_done, 1)

            def gate(g):
                R, p = rows_of(g), g.mod(2)
                pe.wait_ge(yThi_done, g.times(2, 2))
                pe.wait_ge(yTlo_done, g.times(2, 2))
                for t in range(T):
                    s = slice(t * R, (t + 1) * R)
                    dst = ps_x[0][0:R, t * E:(t + 1) * E]
                    for k in range(2):
                        pe.matmul(dst, yT_hi[p][:, k, s], gate_hi[:, k, :], start=(k == 0), stop=False)
                        pe.matmul(dst, yT_hi[p][:, k, s], gate_lo[:, k, :], start=False, stop=False)
                        last = pe.matmul(dst, yT_lo[p][:, k, s], gate_hi[:, k, :], start=False, stop=(k == 1))
                last.then_inc(gate_done, 1)

            def inner_products(g, e):
                N, p, b = T * rows_of(g), g.mod(2), (g.c + e) % 2
                if e == 0:
                    pe.wait_ge(yThi_done, g.times(2, 2))
                    pe.wait_ge(yTlo_done, g.times(2, 2))
                if reached(g.times(NE, e - 1)):
                    pe.wait_ge(mul_done, g.times(NE, e - 1))
                for w, bank in ((0, ps_h1[b]), (1, ps_h3[b])):
                    for k in range(2):
                        pe.matmul(bank[:, 0:N], w13_hi[:, k, e, w, :], yT_hi[p][:, k, 0:N],
                                  start=(k == 0), stop=False)
                        pe.matmul(bank[:, 0:N], w13_hi[:, k, e, w, :], yT_lo[p][:, k, 0:N], start=False, stop=False)
                        last = pe.matmul(bank[:, 0:N], w13_lo[:, k, e, w, :], yT_hi[p][:, k, 0:N],
                                         start=False, stop=(k == 1))
                last.then_inc(inner_done, 1)

            def outer_products(g, e):
                R, b = rows_of(g), (g.c + e) % 2
                pe.wait_ge(inlo_done, g.times(NE, e + 1))
                for half_no in range(2):
                    if reached(g.times(2 * NE, 2 * e + half_no - 1)):
                        pe.wait_ge(acc_done, g.times(2 * NE, 2 * e + half_no - 1))
                    for u in range(2):
                        t = 2 * half_no + u
                        s = slice(t * R, (t + 1) * R)
                        dst = ps_y[half_no][0:R, u * C:(u + 1) * C]
                        pe.matmul(dst, in_hi[b][:, s], w2_hi[:, e, :], start=True, stop=False)
                        pe.matmul(dst, in_hi[b][:, s], w2_lo[:, e, :], start=False, stop=False)
                        last = pe.matmul(dst, in_lo[b][:, s], w2_hi[:, e, :], start=False, stop=True)
                    last.then_inc(y_done, 1)

            first = Index(0, 0, 2, GROUPS_B)
            transposes(first)
            gate(first)

            def body(g):
                following = g.back(-1)
                for e in range(NE):
                    inner_products(g, e)
                    if e > 0:
                        outer_products(g, e - 1)
                    elif g.back(1).active():
                        outer_products(g.back(1), NE - 1)
                    if e == 4 and following.active():
                        transposes(following)
                    if e == 6 and following.active():
                        gate(following)
                if not following.active():
                    outer_products(g, NE - 1)
            run(pe.Fori, body)

        @block.scalar
        def _(act):
            def yT_out(g):
                N, p = T * rows_of(g), g.mod(2)
                act.wait_ge(yT_done, g.times(1, 1))
                for k in range(2):
                    act.activation(yT_hi[p][:, k, 0:N], ps_x[k][0:KC, 0:N], ACT.Copy,
                                   scale=SX).then_inc(yThi_done, 1)

            def gate_out(g):
                R = rows_of(g)
                act.wait_ge(gate_done, g.times(1, 1))
                act.activation(half[0:R], ps_x[0][0:R, 0:T * E].rearrange("p (t e) -> p t e", e=E), ACT.Tanh,
                               scale=0.5 / SS).then_inc(tanh_done, 1)

            def silu(g, e):
                N, b = T * rows_of(g), (g.c + e) % 2
                act.wait_ge(inner_done, g.times(NE, e + 1))
                if reached(g.times(NE, e - 1)):
                    act.wait_ge(mul_done, g.times(NE, e - 1))
                act.activation(act1[b][:, 0:N], ps_h1[b][:, 0:N], ACT.Silu, scale=1.0 / SS).then_inc(silu_done, 1)

            def inner_first(g, e):
                N, b = T * rows_of(g), (g.c + e) % 2
                act.wait_ge(mul_done, g.times(NE, e + 1))
                if reached(g.times(2 * NE, 2 * e - 2)):
                    act.wait_ge(y_done, g.times(2 * NE, 2 * e - 2))
                act.activation(in_hi[b][:, 0:N], inner[b][:, 0:N], ACT.Copy).then_inc(inhi_done, 1)

            first = Index(0, 0, 2, GROUPS_B)
            yT_out(first)
            gate_out(first)

            def body(g):
                following = g.back(-1)
                for e in range(NE):
                    silu(g, e)
                    inner_first(g, e)
                    if e == 5 and following.active():
                        yT_out(following)
                    if e == 7 and following.active():
                        gate_out(following)
            run(act.Fori, body)

        @block.vector
        def _(dve):
            settled = sem("dve_settled_b")

            def stats_of(g):
                R, p = rows_of(g), g.mod(2)
                dve.wait_ge(acc_in[p], g.halves(16, 16))
                for t in range(T):
                    dve.bn_stats(bstats[0:R, t, :], acc[p][0:R, t, :]).then_inc(bst_done, 1)
                dve.wait_ge(bst_done, g.times(T, T))
                settle(dve, settled)
                for t in range(T):
                    dve.bn_aggr(bmv[0:R, t, :], bstats[0:R, t, :]).then_inc(bmv_done, 1)

            def normalise(g):
                R, p = rows_of(g), g.mod(2)
                dve.wait_ge(brstd_done, g.times(1, 1))
                if reached(g.times(1)):
                    dve.wait_ge(yT_done, g.times(1))
                for t in range(T):
                    last = dve.tensor_scalar(bnorm[0:R, t, :], acc[p][0:R, t, :], bmv[0:R, t, 0:1],
                                             brstd[0:R, t:t + 1], ALU.subtract, ALU.mult)
                last.then_inc(bnorm_done, 1)

            def yT_out(g):
                N, p = T * rows_of(g), g.mod(2)
                for k in range(2):
                    dve.wait_ge(yThi_done, g.times(2, k + 1))
                    dve.scalar_tensor_tensor(out=yT_lo[p][:, k, 0:N], in0=ps_x[k][0:KC, 0:N], scalar=SX,
                                             in1=yT_hi[p][:, k, 0:N], op0=ALU.mult,
                                             op1=ALU.subtract).then_inc(yTlo_done, 1)

            def route(g):
                R, p = rows_of(g), g.mod(2)
                r = slice(0, R)
                dve.wait_ge(tanh_done, g.times(1, 1))
                n = [0]

                def then(ins):
                    n[0] += 1
                    ins.then_inc(route_step, 1)
                    dve.wait_ge(route_step, g.times(ROUTE_STEPS, n[0]))

                then(dve.tensor_scalar(score[r], half[r], 0.5, 0.5, ALU.mult, ALU.add))
                then(dve.tensor_tensor(biased[r], score[r], gbias[r], ALU.add))
                pairs = biased[r].rearrange("p t (g two) -> p t g two", two=2)
                then(dve.tensor_tensor(gsum[r], pairs[:, :, :, 0], pairs[:, :, :, 1], ALU.add))

                def ranks(values, cmp, eq, before, rank, M):
                    for t in range(T):
                        of_j = values[r, t, :].unsqueeze(1).broadcast_to([R, M, M])
                        of_i = values[r, t, :].unsqueeze(2).broadcast_to([R, M, M])
                        dve.tensor_tensor(cmp[r, t], of_j, of_i, ALU.is_gt)
                        last = dve.tensor_tensor(eq[r, t], of_j, of_i, ALU.is_equal)
                    then(last)
                    for t in range(T):
                        last = dve.tensor_tensor(eq[r, t], eq[r, t], before[r], ALU.mult)
                    then(last)
                    then(dve.tensor_tensor(cmp[r].rearrange("p t i j -> p (t i j)"),
                                           cmp[r].rearrange("p t i j -> p (t i j)"),
                                           eq[r].rearrange("p t i j -> p (t i j)"), ALU.add))
                    then(dve.tensor_reduce(rank[r].rearrange("p t i -> p (t i)"),
                                           cmp[r].rearrange("p t i j -> p (t i) j"), AX.X, ALU.add))

                ranks(gsum, cmp4, eq4, bef4, rank4, G)
                then(dve.tensor_scalar(chosen4[r], rank4[r], 1.5, None, ALU.is_lt))
                then(dve.tensor_scalar(drop4[r], chosen4[r], 1e30, -1e30, ALU.mult, ALU.add))
                by_two = [x[r].rearrange("p t g -> p (t g)").unsqueeze(2).broadcast_to([R, T * G, 2])
                          for x in (chosen4, drop4)]
                in_groups = [x[r].rearrange("p t (g two) -> p (t g) two", two=2) for x in (biased, masked)]
                then(dve.tensor_tensor(in_groups[1], in_groups[0], by_two[0], ALU.mult))
                then(dve.tensor_tensor(in_groups[1], in_groups[1], by_two[1], ALU.add))
                ranks(masked, cmp8, eq8, bef8, rank8, E)
                then(dve.scalar_tensor_tensor(out=wsel[r], in0=rank8[r], scalar=1.5, in1=score[r],
                                              op0=ALU.is_lt, op1=ALU.mult))
                then(dve.tensor_reduce(den[r], wsel[r], AX.X, ALU.add))
                then(dve.tensor_scalar(den[r], den[r], 1e-6, SS / SX * SA, ALU.add, ALU.mult))
                then(dve.reciprocal(rden[r], den[r]))
                assert n[0] == ROUTE_STEPS
                dve.tensor_tensor(comb[p][r], wsel[r], rden[r].unsqueeze(2).broadcast_to([R, T, E]),
                                  ALU.mult).then_inc(route_done, 1)

            ROUTE_STEPS = 19

            def multiply(g, e):
                N, b = T * rows_of(g), (g.c + e) % 2
                dve.wait_ge(silu_done, g.times(NE, e + 1))
                if reached(g.times(NE, e - 1)):
                    dve.wait_ge(inhi_done, g.times(NE, e - 1))
                dve.scalar_tensor_tensor(out=inner[b][:, 0:N], in0=ps_h3[b][:, 0:N], scalar=SA / SS,
                                         in1=act1[b][:, 0:N], op0=ALU.mult, op1=ALU.mult).then_inc(mul_done, 1)

            def inner_rest(g, e):
                N, b = T * rows_of(g), (g.c + e) % 2
                dve.wait_ge(inhi_done, g.times(NE, e + 1))
                dve.tensor_tensor(in_lo[b][:, 0:N], inner[b][:, 0:N], in_hi[b][:, 0:N],
                                  ALU.subtract).then_inc(inlo_done, 1)

            def accumulate(g, e):
                R, p = rows_of(g), g.mod(2)
                if e == 0:
                    dve.wait_ge(route_done, g.times(1, 1))
                if reached(g.times(2 * NE, 2 * e)):
                    dve.wait_ge(acc_done, g.times(2 * NE, 2 * e))
                for half_no in range(2):
                    dve.wait_ge(y_done, g.times(2 * NE, 2 * e + half_no + 1))
                    if e < EXPERTS:
                        for u in range(2):
                            t = 2 * half_no + u
                            last = dve.scalar_tensor_tensor(
                                out=acc[p][0:R, t, :], in0=ps_y[half_no][0:R, u * C:(u + 1) * C],
                                scalar=comb[p][0:R, t, e:e + 1], in1=acc[p][0:R, t, :],
                                op0=ALU.mult, op1=ALU.add)
                    else:
                        two = acc[p][0:R, 2 * half_no:2 * half_no + 2, :].rearrange("p t c -> p (t c)")
                        last = dve.scalar_tensor_tensor(out=two, in0=ps_y[half_no][0:R, 0:2 * C],
                                                        scalar=1.0 / (SA * SW), in1=two,
                                                        op0=ALU.mult, op1=ALU.add)
                    last.then_inc(acc_done, 1)

            first = Index(0, 0, 2, GROUPS_B)
            stats_of(first)
            normalise(first)
            yT_out(first)
            route(first)

            def body(g):
                following = g.back(-1)
                for e in range(NE):
                    multiply(g, e)
                    inner_rest(g, e)
                    if e > 0:
                        accumulate(g, e - 1)
                    elif g.back(1).active():
                        accumulate(g.back(1), NE - 1)
                    if following.active():
                        if e == 2:
                            stats_of(following)
                        if e == 3:
                            normalise(following)
                        if e == 5:
                            yT_out(following)
                        if e == 7:
                            route(following)
                if not following.active():
                    accumulate(g, NE - 1)
            run(dve.Fori, body)

        @block.gpsimd
        def _(pool):
            settled = sem("pool_settled_b")

            def rstds(g):
                R = rows_of(g)
                pool.wait_ge(bmv_done, g.times(T, T))
                settle(pool, settled)
                pool.tensor_scalar(bvareps[0:R], bmv[0:R, :, 1], EPS, None, ALU.add).then_inc(bve_done, 1)
                pool.wait_ge(bve_done, g.times(1, 1))
                pool.tensor_tensor(brstd[0:R], bvareps[0:R], minus_half[0:R], ALU.pow).then_inc(brstd_done, 1)

            rstds(Index(0, 0, 2, GROUPS_B))

            def body(g):
                if g.back(-1).active():
                    rstds(g.back(-1))
            run(pool.Fori, body)


def kernel(x, L0_tok_W_lin, L0_tok_b_lin, L0_tok_cls_token, L0_attn_qkv_weight, L0_attn_proj_weight,
           L0_ffn_gate_weight, L0_ffn_gate_bias, L0_ffn_w1, L0_ffn_w2, L0_ffn_w3, L0_ffn_sw1, L0_ffn_sw2,
           L0_ffn_sw3):
    import numpy as np
    import concourse.bacc as bacc
    from concourse.bass_utils import run_bass_kernel_spmd

    pixels = np.asarray(x).reshape(IMAGES, CHANNELS, GRID, PS, GRID, PS).transpose(0, 1, 3, 5, 2, 4)
    pixels = pixels.reshape(IMAGES, PCHUNKS, 128, PATCHES).transpose(0, 2, 1, 3)
    xp = np.zeros((IMAGES, 128, PCHUNKS, SLOTS), np.float32)
    xp[..., 0:TR] = pixels[..., 0:TR]
    xp[..., TR:SLOTS - 1] = pixels[..., TR - 1:PATCHES]

    def chunked(w, rows):
        w = np.asarray(w).T
        return np.ascontiguousarray(w.reshape(w.shape[0] // rows, rows, w.shape[1]).transpose(1, 0, 2))

    bias_cls = np.empty((TR, 2, C), np.float32)
    bias_cls[:] = np.asarray(L0_tok_b_lin)
    bias_cls[TR - 1, 1] = np.asarray(L0_tok_cls_token)[0]
    w1 = np.concatenate([np.asarray(L0_ffn_w1), np.asarray(L0_ffn_sw1)[None]])
    w3 = np.concatenate([np.asarray(L0_ffn_w3), np.asarray(L0_ffn_sw3)[None]])
    w2 = np.concatenate([np.asarray(L0_ffn_w2), np.asarray(L0_ffn_sw2)[None]])
    w13 = np.stack([w1, w3], 1).reshape(NE, 2, INTER, 2, KC).transpose(4, 3, 0, 1, 2)
    gate_bias = np.empty((128, LANES, EXPERTS), np.float32)
    gate_bias[:] = np.asarray(L0_ffn_gate_bias)

    def before(m):
        return np.ascontiguousarray(np.broadcast_to(np.tril(np.ones((m, m), np.float32), -1), (128, m, m)))

    arrays = {
        "xp": xp, "w_lin": chunked(L0_tok_W_lin, 128), "bias_cls": bias_cls,
        "w_qkv": chunked(L0_attn_qkv_weight, KC), "w_proj": chunked(L0_attn_proj_weight, KC),
        "w_gate": chunked(L0_ffn_gate_weight, KC), "gate_bias": gate_bias,
        "w13": np.ascontiguousarray(w13), "w2": np.ascontiguousarray(w2.transpose(2, 0, 1)),
        "ident": np.eye(128, dtype=np.float32), "before4": before(EGROUPS), "before8": before(EXPERTS),
    }
    nc = bacc.Bacc("TRN2", target_bir_lowering=False, num_devices=1)
    ins = [nc.dram_tensor(n, a.shape, F32, kind="ExternalInput").ap() for n, a in arrays.items()]
    out = nc.dram_tensor("out", (IMAGES, TOKENS, C), F32, kind="ExternalOutput").ap()
    vit_layer(nc, *ins, out)
    r = run_bass_kernel_spmd(nc, [arrays], core_ids=[0])
    return r.results[0]["out"]
```

```python
from contextlib import ExitStack

import concourse.bass as bass
from concourse import mybir

F32 = mybir.dt.float32
F16 = mybir.dt.float16
ACT = mybir.ActivationFunctionType
ALU = mybir.AluOpType
AX = mybir.AxisListType

IMAGES = 64
CHANNELS, SIDE, GRID = 3, 224, 14
PS = SIDE // GRID
PATCHES = GRID * GRID
TOKENS = PATCHES + 1
PCHUNKS = CHANNELS * PS * PS // 128
TR = 99
SLOTS = 2 * TR
KEYS = (TR - 1, TR)
C = 192
KC = C // 2
HEADS, D = 12, 16
PAIRS = HEADS // 2
GROUPS = 2 * PAIRS
QB = 64
TRIO = 3
TRIOS = HEADS // TRIO
TB = TRIO * (2 * D + 1)
EXPERTS, INTER = 8, 128
NE = EXPERTS + 1
EGROUPS = 4
TOTAL = IMAGES * TOKENS
LANES = 4
GT = 128 * LANES
FULL = TOTAL // GT
REST = (TOTAL - FULL * GT) // LANES

SX = 64.0
SW = 256.0
SS = SX * SW
SV = 16.0
SQ = 16.0
SA = 64.0
EPS = 1e-5
UNROLL = 4


def reached(value):
    return not isinstance(value, int) or value > 0


def settle(eng, settled):
    eng.sem_inc(settled, 1)


class Index:

    def __init__(self, i, c, unroll=UNROLL, limit=IMAGES):
        self.i, self.c, self.unroll, self.limit = i, c, unroll, limit

    def back(self, d):
        return Index(self.i, self.c - d, self.unroll, self.limit)

    @property
    def known(self):
        return isinstance(self.i, int)

    def active(self):
        return not self.known or 0 <= self.unroll * self.i + self.c < self.limit

    def times(self, per, plus=0):
        return self.i * (self.unroll * per) + (self.c * per + plus)

    def halves(self, per, plus=0):
        return self.i * (self.unroll // 2 * per) + (self.c // 2 * per + plus)

    def mod(self, m):
        return self.c % m


def vit_layer(nc, xp, w_lin, bias_cls, w_qkv, w_proj, w_gate, gate_bias, w13, w2,
              ident, before4, before8, out):
    hidden_dram = nc.dram_tensor("hidden_dram", [IMAGES, TOKENS, C], F32).ap()
    with ExitStack() as ctx:
        def sb(name, shape, dt=F32):
            return ctx.enter_context(nc.sbuf_tensor(name, shape, dt))

        def sem(name):
            return ctx.enter_context(nc.semaphore(name))

        with ExitStack():
            def stage(name, shape):
                return sb(name, shape)

            def split_pair(name, shape):
                return sb(name + "_hi", shape, F16), sb(name + "_lo", shape, F16)

            lin_hi, lin_lo = split_pair("lin", [128, PCHUNKS, C])
            qkv_hi, qkv_lo = split_pair("qkv", [KC, 2, 3 * C])
            proj_hi, proj_lo = split_pair("proj", [KC, 2, C])
            gate_hi, gate_lo = split_pair("gate", [KC, 2, EXPERTS])
            w13_hi, w13_lo = split_pair("w13", [KC, 2, NE, 2, INTER])
            w2_hi, w2_lo = split_pair("w2", [INTER, NE, C])
            id32 = sb("id32", [128, 128])
            id16 = sb("id16", [128, 128], F16)
            biascls = sb("biascls", [TR, 2, C])
            gbias = sb("gbias", [128, LANES, EXPERTS])
            bef4 = sb("bef4", [128, EGROUPS, EGROUPS])
            bef8 = sb("bef8", [128, EXPERTS, EXPERTS])
            eps = sb("eps", [128, 1])
            minus_half = sb("minus_half", [128, LANES])
            eps_qk = sb("eps_qk", [128, 1])

            lin_f = stage("lin_f", [128, PCHUNKS, C])
            qkv_f = stage("qkv_f", [KC, 2, 3 * C])
            proj_f = stage("proj_f", [KC, 2, C])
            gate_f = stage("gate_f", [KC, 2, EXPERTS])
            w13_f = stage("w13_f", [KC, 2, NE, 2, INTER])
            w2_f = stage("w2_f", [INTER, NE, C])
            qk_mean = stage("qk_mean", [KC, 2, 2 * HEADS])
            weights = [(lin_f, lin_hi, lin_lo, w_lin), (qkv_f, qkv_hi, qkv_lo, w_qkv),
                       (proj_f, proj_hi, proj_lo, w_proj), (gate_f, gate_hi, gate_lo, w_gate),
                       (w13_f, w13_hi, w13_lo, w13), (w2_f, w2_hi, w2_lo, w2)]
            others = [(id32, ident), (biascls, bias_cls), (gbias, gate_bias), (bef4, before4), (bef8, before8)]

            xin = [sb(f"xin{p}", [128, PCHUNKS, SLOTS]) for p in range(2)]
            x_hi = [sb(f"x_hi{p}", [128, PCHUNKS, SLOTS], F16) for p in range(2)]
            x_lo = [sb(f"x_lo{p}", [128, PCHUNKS, SLOTS], F16) for p in range(2)]
            h = [sb(f"h{p}", [TR, 2, C]) for p in range(4)]
            stats = sb("stats", [TR, 2, 6])
            meanvar = sb("meanvar", [TR, 2, 2])
            h_rstd = sb("h_rstd", [TR, 2])
            h_lnvar = sb("h_lnvar", [TR, 2])
            xnorm = sb("xnorm", [TR, 2, C])
            xT_hi = sb("xT_hi", [KC, 2, SLOTS], F16)
            xT_lo = sb("xT_lo", [KC, 2, SLOTS], F16)
            qk_sq = sb("qk_sq", [TR, 2 * HEADS, D])
            qk_var = sb("qk_var", [TR, 2 * HEADS])
            qk_lnvar = sb("qk_lnvar", [TR, 2 * HEADS])
            qk_rstd = sb("qk_rstd", [TR, 2 * HEADS])
            qk_norm = [sb(f"qk_norm{t}", [TR, 2 * HEADS, D]) for t in range(2)]
            qk_split = [sb(f"qk_split{t}", [TR, 2 * HEADS, QB], F16) for t in range(2)]
            qT = [sb(f"qT{p}", [128, PAIRS, SLOTS], F16) for p in range(2)]
            kT = [[sb(f"kT{p}{hh}", [128, PAIRS, SLOTS], F16) for hh in range(2)] for p in range(2)]
            v_f = sb("v_f", [TR, 2, HEADS, D])
            v = [sb(f"v{p}", [TR, 2, HEADS, TB], F16) for p in range(2)]
            prob = [sb(f"prob{r}", [TR, 2, SLOTS]) for r in range(4)]
            prob_hi = [sb(f"prob_hi{r}", [TR, 2, SLOTS], F16) for r in range(4)]
            prob_lo = [sb(f"prob_lo{r}", [TR, 2, SLOTS], F16) for r in range(4)]
            oT = sb("oT", [TB, TRIOS, SLOTS])
            o_sum = sb("o_sum", [TR, 2, HEADS, D])
            o_rden = sb("o_rden", [TR, 2, HEADS])
            o_norm = sb("o_norm", [TR, 2, C])
            onT_hi = sb("onT_hi", [KC, 2, SLOTS], F16)
            onT_lo = sb("onT_lo", [KC, 2, SLOTS], F16)
            h2 = [sb(f"h2{p}", [TR, 2, C]) for p in range(2)]

            w_loaded = [sem(f"w_loaded{n}") for n in range(len(weights))]
            consts_loaded = sem("consts_loaded")
            w_centred = sem("w_centred")
            w_hi_done = sem("w_hi_done")
            w_lo_done = sem("w_lo_done")
            consts_set = sem("consts_set")
            v_zeroed = sem("v_zeroed")

            with nc.Block() as block:
                @block.sync
                def _(sp):
                    for n, (f, _, _, dram) in enumerate(weights):
                        sp.dma_start(f[:], dram).then_inc(w_loaded[n], 16)
                    for tile, dram in others:
                        sp.dma_start(tile[:], dram).then_inc(consts_loaded, 16)
                    sp.wait_ge(consts_loaded, 16 * len(others))

                @block.scalar
                def _(act):
                    for n, (f, hi, _, _) in enumerate(weights):
                        act.wait_ge(w_loaded[n], 16)
                        if n == 1:
                            act.wait_ge(w_centred, 3)
                        act.activation(hi[:], f[:], ACT.Copy, scale=SW).then_inc(w_hi_done, 1)
                    act.wait_ge(consts_loaded, 16 * len(others))
                    act.activation(id16[:], id32[:], ACT.Copy).then_inc(consts_set, 1)

                @block.vector
                def _(dve):
                    dve.wait_ge(w_loaded[1], 16)
                    for k in range(2):
                        qk = qkv_f[:, k, 0:2 * C].rearrange("p (h d) -> p h d", d=D)
                        dve.tensor_reduce(qk_mean[:, k, :], qk, AX.X, ALU.add).then_inc(w_centred, 1)
                    dve.wait_ge(w_centred, 2)
                    dve.tensor_scalar(qk_mean[:], qk_mean[:], 1.0 / D, None, ALU.mult).then_inc(w_lo_done, 1)
                    dve.wait_ge(w_lo_done, 1)
                    for k in range(2):
                        qk = qkv_f[:, k, 0:2 * C].rearrange("p (h d) -> p h d", d=D)
                        mean = qk_mean[:, k, :].unsqueeze(2).broadcast_to([KC, 2 * HEADS, D])
                        last = dve.tensor_tensor(qk, qk, mean, ALU.subtract)
                    last.then_inc(w_centred, 1)
                    for n, (f, hi, lo, _) in enumerate(weights):
                        dve.wait_ge(w_hi_done, n + 1)
                        dve.scalar_tensor_tensor(out=lo[:], in0=f[:], scalar=SW, in1=hi[:],
                                                 op0=ALU.mult, op1=ALU.subtract).then_inc(w_lo_done, 1)

                @block.gpsimd
                def _(pool):
                    pool.memset(eps[:], EPS)
                    pool.memset(minus_half[:], -0.5)
                    pool.memset(eps_qk[:], (SS / SQ) ** 2 * EPS)
                    for t in range(2):
                        pool.memset(qk_split[t][:], 0.0)
                    for p in range(2):
                        for hh in range(2):
                            pool.memset(kT[p][hh][:], 0.0)
                        pool.memset(v[p][:], 0.0).then_inc(v_zeroed, 1)
                    pool.wait_ge(v_zeroed, 2)
                    for p in range(2):
                        for i in range(TRIO):
                            of_head = v[p][:].rearrange("p t (g i) e -> p (t g) i e", i=TRIO)[:, :, i, :]
                            at = TRIO * 2 * D + i
                            last = pool.memset(of_head[:, :, at:at + 1], SV)
                    last.then_inc(consts_set, 1)
                    pool.wait_ge(consts_set, 2)

        phase_a(nc, xp, hidden_dram, sem, locals())
        phase_b(nc, hidden_dram, out, sem, sb, locals())


def phase_a(nc, xp, hidden_dram, sem, bufs):
    (lin_hi, lin_lo, qkv_hi, qkv_lo, proj_hi, proj_lo, id32, id16, biascls, eps, eps_qk, xin, x_hi, x_lo,
     h, stats, meanvar, h_rstd, h_lnvar, xnorm, xT_hi, xT_lo, qk_sq, qk_var, qk_lnvar, qk_rstd,
     qk_norm, qk_split, qT, kT, v_f, v, prob, prob_hi, prob_lo, oT, o_sum, o_rden, o_norm, onT_hi, onT_lo, h2) = (
        bufs[n] for n in (
            "lin_hi lin_lo qkv_hi qkv_lo proj_hi proj_lo id32 id16 biascls eps eps_qk xin x_hi x_lo "
            "h stats meanvar h_rstd h_lnvar xnorm xT_hi xT_lo qk_sq qk_var qk_lnvar qk_rstd "
            "qk_norm qk_split qT kT v_f v prob prob_hi prob_lo oT o_sum o_rden o_norm onT_hi onT_lo h2").split())
    with ExitStack() as ctx:
        def ps(name, shape, dt=F32):
            return ctx.enter_context(nc.psum_tensor(name, shape, dt))

        ps_hid = ps("ps_hid", [128, 512])
        ps_tr = ps("ps_tr", [128, 512])
        ps_qk = ps("ps_qk", [128, 512])
        ps_qkT = ps("ps_qkT", [128, 1024], F16)
        ps_sc = [ps(f"ps_sc{b}", [128, 512]) for b in range(2)]
        ps_o = [ps(f"ps_o{t}", [128, 512]) for t in range(2)]
        hid = ps_hid[0:TR, 0:2 * C].rearrange("p (t c) -> p t c", t=2)
        tok = ps_tr[0:TR, 0:2 * C].rearrange("p (t c) -> p t c", t=2)
        o_feat = ps_tr[0:KC, 0:2 * SLOTS].rearrange("p (k s) -> p k s", k=2)
        x_feat = ps_qk[0:KC, 0:2 * SLOTS].rearrange("p (k s) -> p k s", k=2)
        qk_ps = ps_qk[0:TR, 0:2 * C].rearrange("p (h d) -> p h d", d=D)
        TRP = TR + 1
        qkT_ps = ps_qkT[:, 0:PAIRS * TRP].rearrange("p (b s) -> p b s", s=TRP)
        sc = [b[:, 0:2 * SLOTS].rearrange("p (h s) -> p h s", h=2) for b in ps_sc]
        oT_ps = [b[0:TB, 0:2 * SLOTS].rearrange("p (g s) -> p g s", g=2) for b in ps_o]

        x_in = [sem(f"x_in{p}") for p in range(2)]
        h2_out = [sem(f"h2_out{p}") for p in range(2)]
        hid_done, xT_done, qk_done, v_done = sem("hid_done"), sem("xT_done"), sem("qk_done"), sem("v_done")
        qkT_done, sc_done, av_done = sem("qkT_done"), sem("sc_done"), sem("av_done")
        otok_done, onT_done, proj_done = sem("otok_done"), sem("onT_done"), sem("proj_done")
        xhi_done, xThi_done, sq_done, exp_done = sem("xhi_done"), sem("xThi_done"), sem("sq_done"), sem("exp_done")
        qkT_out, vf_done, oT_out, onThi_done = sem("qkT_out"), sem("vf_done"), sem("oT_out"), sem("onThi_done")
        xlo_done, h_done, stats_done, mv_done = sem("xlo_done"), sem("h_done"), sem("stats_done"), sem("mv_done")
        xnorm_done, xTlo_done, qkvar_done, qknorm_done = (
            sem("xnorm_done"), sem("xTlo_done"), sem("qkvar_done"), sem("qknorm_done"))
        phi0_done, phi1_done, plo_done = sem("phi0_done"), sem("phi1_done"), sem("plo_done")
        o_read, rden_done, onorm_done, onTlo_done, h2_done = (
            sem("o_read"), sem("rden_done"), sem("onorm_done"), sem("onTlo_done"), sem("h2_done"))
        hln_done, hrstd_done, qkln_done, qkrstd_done, qkhi_done = (
            sem("hln_done"), sem("hrstd_done"), sem("qkln_done"), sem("qkrstd_done"), sem("qkhi_done"))
        qksplit_done = sem("qksplit_done")
        vhi_done, vsplit_done = sem("vhi_done"), sem("vsplit_done")

        def run(fori, step):
            first = 2
            for k in range(first * UNROLL):
                step(Index(0, k))
            with fori(first, IMAGES // UNROLL) as i:
                for c in range(UNROLL):
                    step(Index(i, c))
            for k in range(IMAGES, IMAGES + 5):
                step(Index(0, k))

        block = ctx.enter_context(nc.Block())

        @block.sync
        def _(sp):
            def load(n):
                p = n.mod(2)
                if reached(n.times(1, -1)):
                    sp.wait_ge(xhi_done, n.times(1, -1))
                if reached(n.times(1, -1)):
                    sp.wait_ge(xlo_done, n.times(1, -1))
                sp.dma_start(xin[p][:], xp[n.times(1)]).then_inc(x_in[p], 16)

            def store(n):
                p = n.mod(2)
                sp.wait_ge(h2_done, n.times(1, 1))
                image = hidden_dram[n.times(1)]
                sp.dma_start(image[1:TOKENS].rearrange("(t p) c -> p t c", t=2),
                             h2[p][0:TR - 1, :, :]).then_inc(h2_out[p], 16)
                sp.dma_start(image[0:1], h2[p][TR - 1:TR, 1, :]).then_inc(h2_out[p], 16)

            def step(k):
                if k.active():
                    load(k)
                if k.back(5).active():
                    store(k.back(5))

            run(sp.Fori, step)
            for p in range(2):
                sp.wait_ge(h2_out[p], 32 * (IMAGES // 2))

        @block.tensor
        def _(pe):
            def products(outs, lhs, rhs, chunks):
                (lhs_hi, lhs_lo), (rhs_hi, rhs_lo) = lhs, rhs
                for k in range(chunks):
                    pe.matmul(outs, lhs_hi(k), rhs_hi(k), start=(k == 0), stop=False)
                    pe.matmul(outs, lhs_hi(k), rhs_lo(k), start=False, stop=False)
                    last = pe.matmul(outs, lhs_lo(k), rhs_hi(k), start=False, stop=(k == chunks - 1))
                return last

            def embed(n, t):
                p, s = n.mod(2), slice(t * TR, (t + 1) * TR)
                if t == 0:
                    pe.wait_ge(xhi_done, n.times(1, 1))
                    pe.wait_ge(xlo_done, n.times(1, 1))
                    if reached(n.times(1, -1)):
                        pe.wait_ge(vf_done, n.times(1, -1))
                last = products(hid[:, t, :],
                                (lambda k: x_hi[p][:, k, s], lambda k: x_lo[p][:, k, s]),
                                (lambda k: lin_hi[:, k, :], lambda k: lin_lo[:, k, :]), PCHUNKS)
                if t == 1:
                    last.then_inc(hid_done, 1)

            def transpose_tokens(feat, src, done):
                for t in range(2):
                    for k in range(2):
                        last = pe.transpose(feat[:, k, t * TR:(t + 1) * TR], src[:, t, k * KC:(k + 1) * KC],
                                            id32[0:TR, 0:TR])
                last.then_inc(done, 1)

            def from_xT(outs, t, cols):
                s = slice(t * TR, (t + 1) * TR)
                return products(outs, (lambda k: xT_hi[:, k, s], lambda k: xT_lo[:, k, s]),
                                (lambda k: qkv_hi[:, k, cols], lambda k: qkv_lo[:, k, cols]), 2)

            def qk(n, t):
                if t == 0:
                    pe.wait_ge(xThi_done, n.times(1, 1))
                    pe.wait_ge(xTlo_done, n.times(1, 1))
                if reached(n.times(2, t)):
                    pe.wait_ge(qknorm_done, n.times(2, t))
                from_xT(ps_qk[0:TR, 0:2 * C], t, slice(0, 2 * C)).then_inc(qk_done, 1)

            def values(n, embedded):
                if embedded.active():
                    pe.wait_ge(h_done, embedded.times(1, 1))
                for t in range(2):
                    last = from_xT(hid[:, t, :], t, slice(2 * C, 3 * C))
                last.then_inc(v_done, 1)

            def transpose_qk(n, t, w):
                if w == 0:
                    pe.wait_ge(qksplit_done, n.times(2, t + 1))
                if reached(n.times(4, 2 * t + w)):
                    pe.wait_ge(qkT_out, n.times(4, 2 * t + w))
                part = qk_split[t][:, w * HEADS:(w + 1) * HEADS, :].rearrange("p (b h) e -> p b (h e)", h=2)
                for b in range(PAIRS):
                    last = pe.transpose(qkT_ps[:, b, 0:TR], part[:, b, :], id16[0:TR, 0:TR])
                last.then_inc(qkT_done, 1)

            def scores(n, j):
                p, pair, m = n.mod(2), j // 2, j % 2
                if j == 0:
                    pe.wait_ge(qkT_out, n.times(4, 4))
                if reached(n.times(GROUPS, j - 1)):
                    pe.wait_ge(exp_done, n.times(GROUPS, j - 1))
                for hh in range(2):
                    last = pe.matmul(sc[j % 2][0:KEYS[m], hh, :], kT[p][hh][:, pair, m * TR:m * TR + KEYS[m]],
                                     qT[p][:, pair, :], start=True, stop=True)
                last.then_inc(sc_done, 1)

            def attend(n, pair):
                p = n.mod(2)
                if pair == 0:
                    pe.wait_ge(vsplit_done, n.times(1, 1))
                for hh in range(2):
                    trio, place = divmod(2 * pair + hh, TRIO)
                    if place == 0 and trio % 2 == 0:
                        if reached(n.times(2, trio // 2 - 1)):
                            pe.wait_ge(oT_out, n.times(2, trio // 2 - 1))
                    if hh == 0:
                        pe.wait_ge(plo_done, n.times(GROUPS, 2 * pair + 2))
                    dst = oT_ps[trio // 2][:, trio % 2, :]
                    for m in range(2):
                        r, rows = (2 * pair + m) % 4, slice(0, KEYS[m])
                        own = v[p][rows, m, 2 * pair + hh, :]
                        pe.matmul(dst, own, prob_hi[r][rows, hh, :], start=(place == 0 and m == 0), stop=False)
                        last = pe.matmul(dst, own, prob_lo[r][rows, hh, :], start=False,
                                         stop=(place == TRIO - 1 and m == 1))
                last.then_inc(av_done, 1)

            def o_by_token(n, t):
                if t == 0:
                    pe.wait_ge(oT_out, n.times(2, 2))
                else:
                    pe.wait_ge(o_read, n.times(2, 1))
                for g in range(TRIOS):
                    last = pe.transpose(ps_tr[0:TR, g * TB:(g + 1) * TB], oT[:, g, t * TR:(t + 1) * TR],
                                        id32[0:TB, 0:TB])
                last.then_inc(otok_done, 1)

            def project(n):
                pe.wait_ge(onThi_done, n.times(1, 1))
                pe.wait_ge(onTlo_done, n.times(1, 1))
                for t in range(2):
                    s = slice(t * TR, (t + 1) * TR)
                    last = products(tok[:, t, :], (lambda k: onT_hi[:, k, s], lambda k: onT_lo[:, k, s]),
                                    (lambda k: proj_hi[:, k, :], lambda k: proj_lo[:, k, :]), 2)
                last.then_inc(proj_done, 1)

            def step(k):
                n1, n2, n3, n4, n5 = (k.back(d) for d in (1, 2, 3, 4, 5))
                for slot in range(PAIRS):
                    if slot == 2 and n1.active():
                        embed(n1, 1)
                    attended = (n3 if slot > 3 else n4), (slot + 2) % PAIRS
                    if attended[0].active():
                        attend(*attended)
                    scored, pair = (n3 if slot > 1 else n4), (slot - 2) % PAIRS
                    if scored.active():
                        scores(scored, 2 * pair)
                        scores(scored, 2 * pair + 1)
                    if slot < 2 and n3.active():
                        transpose_qk(n3, 1, slot)
                    if slot > 3 and n2.active():
                        transpose_qk(n2, 0, slot - 4)
                    if slot == 0 and n2.active():
                        pe.wait_ge(xnorm_done, n2.times(1, 1))
                        if reached(n2.times(2)):
                            pe.wait_ge(qknorm_done, n2.times(2))
                        transpose_tokens(x_feat, xnorm, xT_done)
                    if slot == 0 and n1.active():
                        embed(n1, 0)
                    if slot == 1 and n5.active():
                        pe.wait_ge(onorm_done, n5.times(1, 1))
                        transpose_tokens(o_feat, o_norm, onT_done)
                    if slot == 1 and n2.active():
                        qk(n2, 0)
                    if slot == 2 and n5.active():
                        project(n5)
                    if slot == 3 and n2.active():
                        qk(n2, 1)
                    if slot == 4 and n2.active():
                        values(n2, n1)
                    if slot == 4 and n4.active():
                        if n5.active():
                            pe.wait_ge(h2_done, n5.times(1, 1))
                        o_by_token(n4, 0)
                    if slot == 5 and n4.active():
                        o_by_token(n4, 1)

            run(pe.Fori, step)

        @block.scalar
        def _(act):
            act.preload_act_table_set("natural_log_exp_and_others")

            def split_x(n):
                p = n.mod(2)
                act.wait_ge(x_in[p], n.halves(16, 16))
                if reached(n.times(1, -1)):
                    act.wait_ge(hid_done, n.times(1, -1))
                act.activation(x_hi[p][:], xin[p][:], ACT.Copy, scale=SX).then_inc(xhi_done, 1)

            def xT_out(n):
                act.wait_ge(xT_done, n.times(1, 1))
                if reached(n.times(1)):
                    act.wait_ge(v_done, n.times(1))
                act.activation(xT_hi[:], x_feat, ACT.Copy, scale=SX).then_inc(xThi_done, 1)

            def square(n, t):
                act.wait_ge(qk_done, n.times(2, t + 1))
                if reached(n.times(2, t)):
                    act.wait_ge(qkvar_done, n.times(2, t))
                act.activation(qk_sq[:], qk_ps, ACT.Square, scale=1.0 / SS).then_inc(sq_done, 1)

            def h_rstds(n):
                act.wait_ge(mv_done, n.times(2, 2))
                act.activation(h_lnvar[:], meanvar[:, :, 1], ACT.Ln, bias=eps[0:TR]).then_inc(hln_done, 1)
                act.wait_ge(hln_done, n.times(1, 1))
                act.activation(h_rstd[:], h_lnvar[:], ACT.Exp, scale=-0.5).then_inc(hrstd_done, 1)

            def qk_rstds(n, t):
                act.wait_ge(qkvar_done, n.times(2, t + 1))
                act.activation(qk_lnvar[:], qk_var[:], ACT.Ln, bias=eps_qk[0:TR],
                               scale=(SS / SQ) ** 2 / D).then_inc(qkln_done, 1)
                act.wait_ge(qkln_done, n.times(2, t + 1))
                act.activation(qk_rstd[:], qk_lnvar[:], ACT.Exp, scale=-0.5).then_inc(qkrstd_done, 1)

            def qk_first(n, t):
                act.wait_ge(qknorm_done, n.times(2, t + 1))
                if reached(n.times(4, 2 * t - 2)):
                    act.wait_ge(qkT_done, n.times(4, 2 * t - 2))
                f, s = qk_norm[t], qk_split[t]
                q, k = slice(0, HEADS), slice(HEADS, 2 * HEADS)
                act.activation(s[:, :, 0:D], f[:], ACT.Copy)
                act.activation(s[:, q, D:2 * D], f[:, q, :], ACT.Copy)
                act.activation(s[:, k, 2 * D:3 * D], f[:, k, :], ACT.Copy).then_inc(qkhi_done, 1)

            def qkT_copy(n, t, w):
                act.wait_ge(qkT_done, n.times(4, 2 * t + w + 1))
                if t == 0:
                    if reached(n.times(GROUPS, -GROUPS)):
                        act.wait_ge(sc_done, n.times(GROUPS, -GROUPS))
                cols = slice(t * TR, (t + 1) * TR)
                if w == 0:
                    act.activation(qT[n.mod(2)][:, :, cols], qkT_ps[:, :, 0:TR], ACT.Copy).then_inc(qkT_out, 1)
                else:
                    for hh in range(2):
                        rows = slice(QB * hh, QB * hh + QB)
                        last = act.activation(kT[n.mod(2)][hh][rows, :, cols], qkT_ps[rows, :, 0:TR], ACT.Copy)
                    last.then_inc(qkT_out, 1)

            def v_copy(n):
                act.wait_ge(v_done, n.times(1, 1))
                if reached(n.times(1)):
                    act.wait_ge(vsplit_done, n.times(1))
                act.activation(v_f[:].rearrange("p t h d -> p (t h d)"), ps_hid[0:TR, 0:2 * C], ACT.Copy,
                               scale=SV / SS).then_inc(vf_done, 1)

            def oT_copy(n, b):
                if reached(n.times(PAIRS, 3 * b + 3)):
                    act.wait_ge(av_done, n.times(PAIRS, 3 * b + 3))
                if reached(n.times(2)):
                    act.wait_ge(otok_done, n.times(2))
                act.activation(oT[:, 2 * b:2 * b + 2, :], oT_ps[b], ACT.Copy).then_inc(oT_out, 1)

            def exponent(n, j):
                rows = slice(0, KEYS[j % 2])
                act.wait_ge(sc_done, n.times(GROUPS, j + 1))
                if reached(n.times(GROUPS, j - 3)):
                    act.wait_ge(plo_done, n.times(GROUPS, j - 3))
                act.activation(prob[j % 4][rows], sc[j % 2][rows], ACT.Exp,
                               scale=D ** -0.5 / (SQ * SQ)).then_inc(exp_done, 1)

            def prob_first(n, j):
                rows, r = slice(0, KEYS[j % 2]), j % 4
                act.wait_ge(exp_done, n.times(GROUPS, j + 1))
                if reached(n.times(PAIRS, j // 2 - 1)):
                    act.wait_ge(av_done, n.times(PAIRS, j // 2 - 1))
                act.activation(prob_hi[r][rows], prob[r][rows], ACT.Copy).then_inc(phi0_done, 1)

            def onT_out(n):
                act.wait_ge(onT_done, n.times(1, 1))
                if reached(n.times(1)):
                    act.wait_ge(proj_done, n.times(1))
                act.activation(onT_hi[:], o_feat, ACT.Copy, scale=SX).then_inc(onThi_done, 1)

            def step(k):
                n1, n2, n3, n4, n5 = (k.back(d) for d in (1, 2, 3, 4, 5))
                for slot in range(PAIRS):
                    if slot == 1 and n4.active():
                        oT_copy(n4, 0)
                    if slot == 4 and n4.active():
                        oT_copy(n4, 1)
                    if slot == 2 and k.active():
                        split_x(k)
                    if slot == 2 and n2.active():
                        qk_rstds(n2, 0)
                    if slot == 5 and n2.active():
                        v_copy(n2)
                    scored, pair = (n3 if slot > 1 else n4), (slot - 2) % PAIRS
                    if scored.active():
                        exponent(scored, 2 * pair)
                        exponent(scored, 2 * pair + 1)
                        prob_first(scored, 2 * pair)
                    if slot < 2 and n3.active():
                        qkT_copy(n3, 1, slot)
                    if slot == 0 and n2.active():
                        xT_out(n2)
                    if slot == 1 and n5.active():
                        onT_out(n5)
                    if slot == 1 and n2.active():
                        square(n2, 0)
                    if slot == 3 and n2.active():
                        qk_first(n2, 0)
                        square(n2, 1)
                    if slot == 4 and n2.active():
                        qk_rstds(n2, 1)
                    if slot == 4 and n1.active():
                        h_rstds(n1)
                    if slot == 5 and n2.active():
                        qk_first(n2, 1)
                    if slot > 3 and n2.active():
                        qkT_copy(n2, 0, slot - 4)

            run(act.Fori, step)

        @block.vector
        def _(dve):
            settled = sem("dve_settled_a")

            def split_x(n):
                p = n.mod(2)
                dve.wait_ge(xhi_done, n.times(1, 1))
                dve.scalar_tensor_tensor(out=x_lo[p][:], in0=xin[p][:], scalar=SX, in1=x_hi[p][:],
                                         op0=ALU.mult, op1=ALU.subtract).then_inc(xlo_done, 1)

            def hidden(n):
                q = n.mod(4)
                dve.wait_ge(hid_done, n.times(1, 1))
                if reached(n.times(1, -3)):
                    dve.wait_ge(h2_done, n.times(1, -3))
                dve.scalar_tensor_tensor(out=h[q][:], in0=hid, scalar=1.0 / SS, in1=biascls[:],
                                         op0=ALU.mult, op1=ALU.add).then_inc(h_done, 1)
                dve.wait_ge(h_done, n.times(1, 1))
                for t in range(2):
                    dve.bn_stats(stats[:, t, :], h[q][:, t, :]).then_inc(stats_done, 1)
                dve.wait_ge(stats_done, n.times(2, 2))
                settle(dve, settled)
                for t in range(2):
                    dve.bn_aggr(meanvar[:, t, :], stats[:, t, :]).then_inc(mv_done, 1)

            def norm_hidden(n):
                dve.wait_ge(hrstd_done, n.times(1, 1))
                if reached(n.times(1)):
                    dve.wait_ge(xT_done, n.times(1))
                for t in range(2):
                    last = dve.tensor_scalar(xnorm[:, t, :], h[n.mod(4)][:, t, :], meanvar[:, t, 0:1],
                                             h_rstd[:, t:t + 1], ALU.subtract, ALU.mult)
                last.then_inc(xnorm_done, 1)

            def xT_out(n):
                dve.wait_ge(xThi_done, n.times(1, 1))
                dve.scalar_tensor_tensor(out=xT_lo[:], in0=x_feat, scalar=SX, in1=xT_hi[:],
                                         op0=ALU.mult, op1=ALU.subtract).then_inc(xTlo_done, 1)

            def qk_variance(n, t):
                dve.wait_ge(sq_done, n.times(2, t + 1))
                dve.tensor_reduce(qk_var[:], qk_sq[:], AX.X, ALU.add).then_inc(qkvar_done, 1)

            def qk_normalise(n, t):
                dve.wait_ge(qkrstd_done, n.times(2, t + 1))
                if reached(n.times(2, t - 1)):
                    dve.wait_ge(qksplit_done, n.times(2, t - 1))
                dve.tensor_tensor(qk_norm[t][:], qk_ps, qk_rstd[:].unsqueeze(2).broadcast_to([TR, 2 * HEADS, D]),
                                  ALU.mult).then_inc(qknorm_done, 1)

            def prob_first(n, j):
                rows, r = slice(0, KEYS[j % 2]), j % 4
                dve.wait_ge(exp_done, n.times(GROUPS, j + 1))
                if reached(n.times(PAIRS, j // 2 - 1)):
                    dve.wait_ge(av_done, n.times(PAIRS, j // 2 - 1))
                dve.tensor_copy(prob_hi[r][rows], prob[r][rows]).then_inc(phi1_done, 1)

            def prob_rest(n, j):
                rows, r = slice(0, KEYS[j % 2]), j % 4
                dve.wait_ge((phi0_done, phi1_done)[j % 2], n.times(PAIRS, j // 2 + 1))
                dve.tensor_tensor(prob_lo[r][rows], prob[r][rows], prob_hi[r][rows],
                                  ALU.subtract).then_inc(plo_done, 1)

            def o_out(n, t):
                dve.wait_ge(otok_done, n.times(2, t + 1))
                trios = ps_tr[0:TR, 0:TRIOS * TB].rearrange("p (g e) -> p g e", e=TB)
                dve.reciprocal(o_rden[:, t, :].rearrange("p (g i) -> p g i", i=TRIO),
                               trios[:, :, TRIO * 2 * D:TB]).then_inc(rden_done, 1)
                parts = trios[:, :, 0:TRIO * 2 * D].rearrange("p g (i two d) -> p g i d two", two=2, d=D)
                dve.tensor_reduce(o_sum[:, t, :, :].rearrange("p (g i) d -> p g i d", i=TRIO), parts,
                                  AX.X, ALU.add).then_inc(o_read, 1)

            def o_normalise(n):
                dve.wait_ge(rden_done, n.times(2, 2))
                dve.wait_ge(o_read, n.times(2, 2))
                if reached(n.times(1)):
                    dve.wait_ge(onT_done, n.times(1))
                dve.tensor_tensor(o_norm[:].rearrange("p t (h d) -> p (t h) d", d=D),
                                  o_sum[:].rearrange("p t h d -> p (t h) d"),
                                  o_rden[:].rearrange("p t h -> p (t h)").unsqueeze(2)
                                  .broadcast_to([TR, 2 * HEADS, D]), ALU.mult).then_inc(onorm_done, 1)

            def onT_out(n):
                dve.wait_ge(onThi_done, n.times(1, 1))
                dve.scalar_tensor_tensor(out=onT_lo[:], in0=o_feat, scalar=SX, in1=onT_hi[:],
                                         op0=ALU.mult, op1=ALU.subtract).then_inc(onTlo_done, 1)

            def residual(n):
                p = n.mod(2)
                dve.wait_ge(proj_done, n.times(1, 1))
                if reached(n.halves(32)):
                    dve.wait_ge(h2_out[p], n.halves(32))
                dve.scalar_tensor_tensor(out=h2[p][:], in0=tok, scalar=1.0 / SS, in1=h[n.mod(4)][:],
                                         op0=ALU.mult, op1=ALU.add).then_inc(h2_done, 1)

            def step(k):
                n1, n2, n3, n4, n5 = (k.back(d) for d in (1, 2, 3, 4, 5))
                for slot in range(PAIRS):
                    if slot == 1 and n2.active():
                        xT_out(n2)
                    if slot == 2 and n2.active():
                        qk_variance(n2, 0)
                    if slot == 2 and n5.active():
                        onT_out(n5)
                    if slot == 4 and n2.active():
                        qk_variance(n2, 1)
                    if slot == 5 and n2.active():
                        qk_normalise(n2, 1)
                    if slot == 5 and n4.active():
                        o_out(n4, 0)
                    split, pair = (n3 if slot > 2 else n4), (slot + 3) % PAIRS
                    if split.active():
                        prob_first(split, 2 * pair + 1)
                        prob_rest(split, 2 * pair)
                        prob_rest(split, 2 * pair + 1)
                    if slot == 0 and n5.active():
                        o_out(n5, 1)
                        o_normalise(n5)
                    if slot == 2 and n2.active():
                        qk_normalise(n2, 0)
                    if slot == 3 and n5.active():
                        residual(n5)
                    if slot == 3 and n1.active():
                        hidden(n1)
                    if slot == 4 and k.active():
                        split_x(k)
                    if slot == 5 and n1.active():
                        norm_hidden(n1)

            run(dve.Fori, step)

        @block.gpsimd
        def _(pool):
            settled = sem("pool_settled_a")

            def qk_rest(n, t):
                pool.wait_ge(qkhi_done, n.times(2, t + 1))
                f, s = qk_norm[t], qk_split[t]
                q, k = slice(0, HEADS), slice(HEADS, 2 * HEADS)
                pool.tensor_tensor(s[:, q, 2 * D:3 * D], f[:, q, :], s[:, q, 0:D], ALU.subtract)
                pool.tensor_tensor(s[:, k, D:2 * D], f[:, k, :], s[:, k, 0:D],
                                   ALU.subtract).then_inc(qksplit_done, 1)

            def split_v(n):
                p = n.mod(2)
                pool.wait_ge(vf_done, n.times(1, 1))
                if reached(n.times(PAIRS, -PAIRS)):
                    pool.wait_ge(av_done, n.times(PAIRS, -PAIRS))
                settle(pool, settled)
                own = [v_at(p, t, 0) for t in range(2)]
                rest = [v_at(p, t, D) for t in range(2)]
                for t in range(2):
                    f = v_f[:, t].rearrange("p (g i) d -> p g i d", i=TRIO)
                    pool.tensor_copy(own[t], f).then_inc(vhi_done, 1)
                pool.wait_ge(vhi_done, n.times(2, 2))
                for t in range(2):
                    f = v_f[:, t].rearrange("p (g i) d -> p g i d", i=TRIO)
                    last = pool.tensor_tensor(rest[t], f, own[t], ALU.subtract)
                last.then_inc(vsplit_done, 1)

            def v_at(p, t, plus):
                tile = v[p][:, t, :, :]
                return bass.AP(tensor=tile.tensor, offset=tile.offset + plus,
                               ap=[[tile.ap[0][0], TR], [TRIO * TB, TRIOS], [TB + 2 * D, TRIO], [1, D]])

            def step(k):
                n2 = k.back(2)
                if n2.active():
                    qk_rest(n2, 0)
                    qk_rest(n2, 1)
                    split_v(n2)

            run(pool.Fori, step)


def phase_b(nc, hidden_dram, out, sem, sb, bufs):
    w13_hi, w13_lo, w2_hi, w2_lo, gate_hi, gate_lo, id32, gbias, bef4, bef8, minus_half = (
        bufs[n] for n in "w13_hi w13_lo w2_hi w2_lo gate_hi gate_lo id32 gbias bef4 bef8 minus_half".split())
    with ExitStack() as ctx:
        def ps(name, shape, dt=F32):
            return ctx.enter_context(nc.psum_tensor(name, shape, dt))

        T, E, G = LANES, EXPERTS, EGROUPS
        hin = [sb(f"hin{p}", [128, T, C]) for p in range(2)]
        acc = [sb(f"acc{p}", [128, T, C]) for p in range(2)]
        bstats = sb("bstats", [128, T, 6])
        bmv = sb("bmv", [128, T, 2])
        bvareps = sb("bvareps", [128, T])
        brstd = sb("brstd", [128, T])
        bnorm = sb("bnorm", [128, T, C])
        yT_hi = [sb(f"yT_hi{p}", [KC, 2, GT], F16) for p in range(2)]
        yT_lo = [sb(f"yT_lo{p}", [KC, 2, GT], F16) for p in range(2)]
        act1 = [sb(f"act1{p}", [INTER, GT]) for p in range(2)]
        inner = [sb(f"inner{p}", [INTER, GT]) for p in range(3)]
        in_hi = [sb(f"in_hi{p}", [INTER, GT], F16) for p in range(3)]
        in_lo = [sb(f"in_lo{p}", [INTER, GT], F16) for p in range(3)]
        half = sb("half", [128, T, E])
        score = sb("score", [128, T, E])
        biased = sb("biased", [128, T, E])
        gsum = sb("gsum", [128, T, G])
        cmp4 = sb("cmp4", [128, T, G, G])
        eq4 = sb("eq4", [128, T, G, G])
        rank4 = sb("rank4", [128, T, G])
        chosen4 = sb("chosen4", [128, T, G])
        drop4 = sb("drop4", [128, T, G])
        masked = sb("masked", [128, T, E])
        cmp8 = sb("cmp8", [128, T, E, E])
        eq8 = sb("eq8", [128, T, E, E])
        rank8 = sb("rank8", [128, T, E])
        wsel = sb("wsel", [128, T, E])
        den = sb("den", [128, T])
        rden = sb("rden", [128, T])
        comb = [sb(f"comb{p}", [128, T, E]) for p in range(2)]

        ps_h1 = [ps(f"ps_h1{b}", [128, 512]) for b in range(2)]
        ps_h3 = [ps(f"ps_h3{b}", [128, 512]) for b in range(2)]
        ps_y = [ps(f"ps_y{b}", [128, 512]) for b in range(2)]
        ps_x = [ps(f"ps_x{k}", [128, 512]) for k in range(2)]

        h_in = [sem(f"h_in{p}") for p in range(2)]
        acc_out = [sem(f"acc_out{p}") for p in range(2)]
        yT_done, gate_done, inner_done, y_done = sem("yT_done"), sem("gate_done"), sem("inner_done"), sem("y_done")
        yThi_done, tanh_done, silu_done, inhi_done = (
            sem("yThi_done"), sem("tanh_done"), sem("silu_done"), sem("inhi_done"))
        bst_done, bmv_done, bnorm_done, yTlo_done = (
            sem("bst_done"), sem("bmv_done"), sem("bnorm_done"), sem("yTlo_done"))
        route_step, route_done = sem("route_step"), sem("route_done")
        mul_done, inlo_done, acc_done = sem("mul_done"), sem("inlo_done"), sem("acc_done")
        bve_done, brstd_done = sem("bve_done"), sem("brstd_done")

        tokens_in = hidden_dram.rearrange("n t c -> (n t) c")
        tokens_out = out.rearrange("n t c -> (n t) c")
        LAST = FULL
        GROUPS_B = FULL + 1

        def rows_of(g):
            return REST if g.known and g.i * 2 + g.c == LAST else 128

        def full(dram):
            return dram[0:FULL * GT].rearrange("(g p t) c -> g p t c", p=128, t=T)

        def part(dram, g):
            if rows_of(g) == 128:
                return full(dram)[g.times(1)]
            return dram[FULL * GT:TOTAL].rearrange("(p t) c -> p t c", t=T)

        def run(fori, body):
            def at(i, c):
                return Index(i, c, 2, GROUPS_B)
            for g in range(3):
                body(at(0, g))
            with fori(1, (FULL - 4) // 2) as i:
                for c in (1, 2):
                    body(at(i, c))
            for g in range(FULL - 3, FULL + 1):
                body(at(0, g))

        block = ctx.enter_context(nc.Block())

        @block.sync
        def _(sp):
            def load(g):
                p = g.mod(2)
                if reached(g.times(2 * NE, 2 - 4 * NE)):
                    sp.wait_ge(acc_done, g.times(2 * NE, 2 - 4 * NE))
                sp.dma_start(hin[p][0:rows_of(g)], part(tokens_in, g)).then_inc(h_in[p], 16)

            def store(g):
                p = g.mod(2)
                sp.wait_ge(acc_done, g.times(2 * NE, 2 * NE))
                sp.dma_start(part(tokens_out, g), acc[p][0:rows_of(g)]).then_inc(acc_out[p], 16)

            load(Index(0, 0, 2, GROUPS_B))
            load(Index(0, 1, 2, GROUPS_B))

            def body(g):
                if g.back(-2).active():
                    load(g.back(-2))
                store(g)
            run(sp.Fori, body)
            sp.wait_ge(acc_out[0], 16 * (FULL // 2 + 1))
            sp.wait_ge(acc_out[1], 16 * (FULL // 2))

        @block.tensor
        def _(pe):
            def transposes(g):
                R = rows_of(g)
                pe.wait_ge(bnorm_done, g.times(1, 1))
                if reached(g.times(1)):
                    pe.wait_ge(tanh_done, g.times(1))
                for k in range(2):
                    for t in range(T):
                        last = pe.transpose(ps_x[k][0:KC, t * R:(t + 1) * R], bnorm[0:R, t, k * KC:(k + 1) * KC],
                                            id32[0:R, 0:R])
                last.then_inc(yT_done, 1)

            def gate(g):
                R, p = rows_of(g), g.mod(2)
                pe.wait_ge(yThi_done, g.times(2, 2))
                pe.wait_ge(yTlo_done, g.times(2, 2))
                for t in range(T):
                    s = slice(t * R, (t + 1) * R)
                    dst = ps_x[0][0:R, t * E:(t + 1) * E]
                    for k in range(2):
                        pe.matmul(dst, yT_hi[p][:, k, s], gate_hi[:, k, :], start=(k == 0), stop=False)
                        pe.matmul(dst, yT_hi[p][:, k, s], gate_lo[:, k, :], start=False, stop=False)
                        last = pe.matmul(dst, yT_lo[p][:, k, s], gate_hi[:, k, :], start=False, stop=(k == 1))
                last.then_inc(gate_done, 1)

            def inner_products(g, e):
                N, p, b = T * rows_of(g), g.mod(2), (g.c + e) % 2
                if e == 0:
                    pe.wait_ge(yThi_done, g.times(2, 2))
                    pe.wait_ge(yTlo_done, g.times(2, 2))
                if reached(g.times(NE, e - 1)):
                    pe.wait_ge(mul_done, g.times(NE, e - 1))
                for w, bank in ((0, ps_h1[b]), (1, ps_h3[b])):
                    for k in range(2):
                        pe.matmul(bank[:, 0:N], w13_hi[:, k, e, w, :], yT_hi[p][:, k, 0:N],
                                  start=(k == 0), stop=False)
                        pe.matmul(bank[:, 0:N], w13_hi[:, k, e, w, :], yT_lo[p][:, k, 0:N], start=False, stop=False)
                        last = pe.matmul(bank[:, 0:N], w13_lo[:, k, e, w, :], yT_hi[p][:, k, 0:N],
                                         start=False, stop=(k == 1))
                last.then_inc(inner_done, 1)

            def outer_products(g, e):
                R, b = rows_of(g), e % 3
                pe.wait_ge(inlo_done, g.times(NE, e + 1))
                for half_no in range(2):
                    if reached(g.times(2 * NE, 2 * e + half_no - 1)):
                        pe.wait_ge(acc_done, g.times(2 * NE, 2 * e + half_no - 1))
                    for u in range(2):
                        t = 2 * half_no + u
                        s = slice(t * R, (t + 1) * R)
                        dst = ps_y[half_no][0:R, u * C:(u + 1) * C]
                        pe.matmul(dst, in_hi[b][:, s], w2_hi[:, e, :], start=True, stop=False)
                        pe.matmul(dst, in_hi[b][:, s], w2_lo[:, e, :], start=False, stop=False)
                        last = pe.matmul(dst, in_lo[b][:, s], w2_hi[:, e, :], start=False, stop=True)
                    last.then_inc(y_done, 1)

            first = Index(0, 0, 2, GROUPS_B)
            transposes(first)
            gate(first)

            def body(g):
                following = g.back(-1)
                for e in range(NE):
                    inner_products(g, e)
                    if e > 1:
                        outer_products(g, e - 2)
                    elif g.back(1).active():
                        outer_products(g.back(1), e + NE - 2)
                    if e == 3 and following.active():
                        transposes(following)
                    if e == 5 and following.active():
                        gate(following)
                if not following.active():
                    outer_products(g, NE - 2)
                    outer_products(g, NE - 1)
            run(pe.Fori, body)

        @block.scalar
        def _(act):
            def yT_out(g):
                N, p = T * rows_of(g), g.mod(2)
                act.wait_ge(yT_done, g.times(1, 1))
                for k in range(2):
                    act.activation(yT_hi[p][:, k, 0:N], ps_x[k][0:KC, 0:N], ACT.Copy,
                                   scale=SX).then_inc(yThi_done, 1)

            def gate_out(g):
                R = rows_of(g)
                act.wait_ge(gate_done, g.times(1, 1))
                act.activation(half[0:R], ps_x[0][0:R, 0:T * E].rearrange("p (t e) -> p t e", e=E), ACT.Tanh,
                               scale=0.5 / SS).then_inc(tanh_done, 1)

            def silu(g, e):
                N, b = T * rows_of(g), (g.c + e) % 2
                act.wait_ge(inner_done, g.times(NE, e + 1))
                if reached(g.times(NE, e - 1)):
                    act.wait_ge(mul_done, g.times(NE, e - 1))
                act.activation(act1[b][:, 0:N], ps_h1[b][:, 0:N], ACT.Silu, scale=1.0 / SS).then_inc(silu_done, 1)

            def inner_first(g, e):
                N, b = T * rows_of(g), e % 3
                act.wait_ge(mul_done, g.times(NE, e + 1))
                if reached(g.times(2 * NE, 2 * e - 4)):
                    act.wait_ge(y_done, g.times(2 * NE, 2 * e - 4))
                act.activation(in_hi[b][:, 0:N], inner[b][:, 0:N], ACT.Copy).then_inc(inhi_done, 1)

            first = Index(0, 0, 2, GROUPS_B)
            yT_out(first)
            gate_out(first)

            def body(g):
                following = g.back(-1)
                for e in range(NE):
                    silu(g, e)
                    inner_first(g, e)
                    if e == 3 and following.active():
                        yT_out(following)
                    if e == 5 and following.active():
                        gate_out(following)
            run(act.Fori, body)

        @block.vector
        def _(dve):
            settled = sem("dve_settled_b")

            def stats_of(g):
                R, p = rows_of(g), g.mod(2)
                dve.wait_ge(h_in[p], g.halves(16, 16))
                for t in range(T):
                    dve.bn_stats(bstats[0:R, t, :], hin[p][0:R, t, :]).then_inc(bst_done, 1)
                dve.wait_ge(bst_done, g.times(T, T))
                settle(dve, settled)
                for t in range(T):
                    dve.bn_aggr(bmv[0:R, t, :], bstats[0:R, t, :]).then_inc(bmv_done, 1)

            def normalise(g):
                R, p = rows_of(g), g.mod(2)
                dve.wait_ge(brstd_done, g.times(1, 1))
                if reached(g.times(1)):
                    dve.wait_ge(yT_done, g.times(1))
                for t in range(T):
                    last = dve.tensor_scalar(bnorm[0:R, t, :], hin[p][0:R, t, :], bmv[0:R, t, 0:1],
                                             brstd[0:R, t:t + 1], ALU.subtract, ALU.mult)
                last.then_inc(bnorm_done, 1)

            def yT_out(g):
                N, p = T * rows_of(g), g.mod(2)
                for k in range(2):
                    dve.wait_ge(yThi_done, g.times(2, k + 1))
                    dve.scalar_tensor_tensor(out=yT_lo[p][:, k, 0:N], in0=ps_x[k][0:KC, 0:N], scalar=SX,
                                             in1=yT_hi[p][:, k, 0:N], op0=ALU.mult,
                                             op1=ALU.subtract).then_inc(yTlo_done, 1)

            ROUTE_STEPS = 19
            ROUTE_PARTS = (0, 3, 7, 11, 15, ROUTE_STEPS)

            def route(g, part_no):
                R, p = rows_of(g), g.mod(2)
                r = slice(0, R)
                n = [ROUTE_PARTS[part_no]]

                def then(ins):
                    n[0] += 1
                    ins.then_inc(route_step, 1)
                    dve.wait_ge(route_step, g.times(ROUTE_STEPS, n[0]))

                def ranks(values, cmp, eq, before, rank, M):
                    of_j = values[r].unsqueeze(2).broadcast_to([R, T, M, M])
                    of_i = values[r].unsqueeze(3).broadcast_to([R, T, M, M])
                    dve.tensor_tensor(cmp[r], of_j, of_i, ALU.is_gt)
                    then(dve.tensor_tensor(eq[r], of_j, of_i, ALU.is_equal))
                    then(dve.tensor_tensor(eq[r].rearrange("p t i j -> p t (i j)"),
                                           eq[r].rearrange("p t i j -> p t (i j)"),
                                           before[r].rearrange("p i j -> p (i j)").unsqueeze(1)
                                           .broadcast_to([R, T, M * M]), ALU.mult))
                    then(dve.tensor_tensor(cmp[r].rearrange("p t i j -> p (t i j)"),
                                           cmp[r].rearrange("p t i j -> p (t i j)"),
                                           eq[r].rearrange("p t i j -> p (t i j)"), ALU.add))
                    then(dve.tensor_reduce(rank[r].rearrange("p t i -> p (t i)"),
                                           cmp[r].rearrange("p t i j -> p (t i) j"), AX.X, ALU.add))

                if part_no == 0:
                    dve.wait_ge(tanh_done, g.times(1, 1))
                    then(dve.tensor_scalar(score[r], half[r], 0.5, 0.5, ALU.mult, ALU.add))
                    then(dve.tensor_tensor(biased[r], score[r], gbias[r], ALU.add))
                    pairs = biased[r].rearrange("p t (g two) -> p t g two", two=2)
                    then(dve.tensor_tensor(gsum[r], pairs[:, :, :, 0], pairs[:, :, :, 1], ALU.add))
                if part_no == 1:
                    ranks(gsum, cmp4, eq4, bef4, rank4, G)
                if part_no == 2:
                    then(dve.tensor_scalar(chosen4[r], rank4[r], 1.5, None, ALU.is_lt))
                    then(dve.tensor_scalar(drop4[r], chosen4[r], 1e30, -1e30, ALU.mult, ALU.add))
                    by_two = [x[r].rearrange("p t g -> p (t g)").unsqueeze(2).broadcast_to([R, T * G, 2])
                              for x in (chosen4, drop4)]
                    in_groups = [x[r].rearrange("p t (g two) -> p (t g) two", two=2) for x in (biased, masked)]
                    then(dve.tensor_tensor(in_groups[1], in_groups[0], by_two[0], ALU.mult))
                    then(dve.tensor_tensor(in_groups[1], in_groups[1], by_two[1], ALU.add))
                if part_no == 3:
                    ranks(masked, cmp8, eq8, bef8, rank8, E)
                if part_no == 4:
                    then(dve.scalar_tensor_tensor(out=wsel[r], in0=rank8[r], scalar=1.5, in1=score[r],
                                                  op0=ALU.is_lt, op1=ALU.mult))
                    then(dve.tensor_reduce(den[r], wsel[r], AX.X, ALU.add))
                    then(dve.tensor_scalar(den[r], den[r], 1e-6, SS / SX * SA, ALU.add, ALU.mult))
                    then(dve.reciprocal(rden[r], den[r]))
                    dve.tensor_tensor(comb[p][r], wsel[r], rden[r].unsqueeze(2).broadcast_to([R, T, E]),
                                      ALU.mult).then_inc(route_done, 1)
                assert n[0] == ROUTE_PARTS[part_no + 1]

            def multiply(g, e):
                N, b = T * rows_of(g), (g.c + e) % 2
                dve.wait_ge(silu_done, g.times(NE, e + 1))
                if reached(g.times(NE, e - 2)):
                    dve.wait_ge(inlo_done, g.times(NE, e - 2))
                dve.scalar_tensor_tensor(out=inner[e % 3][:, 0:N], in0=ps_h3[b][:, 0:N], scalar=SA / SS,
                                         in1=act1[b][:, 0:N], op0=ALU.mult, op1=ALU.mult).then_inc(mul_done, 1)

            def inner_rest(g, e):
                N, b = T * rows_of(g), e % 3
                dve.wait_ge(inhi_done, g.times(NE, e + 1))
                dve.tensor_tensor(in_lo[b][:, 0:N], inner[b][:, 0:N], in_hi[b][:, 0:N],
                                  ALU.subtract).then_inc(inlo_done, 1)

            def accumulate(g, e):
                R, p = rows_of(g), g.mod(2)
                if e == 0:
                    dve.wait_ge(route_done, g.times(1, 1))
                    if reached(g.halves(16)):
                        dve.wait_ge(acc_out[p], g.halves(16))
                before = hin[p] if e == 0 else acc[p]
                if reached(g.times(2 * NE, 2 * e)):
                    dve.wait_ge(acc_done, g.times(2 * NE, 2 * e))
                for half_no in range(2):
                    dve.wait_ge(y_done, g.times(2 * NE, 2 * e + half_no + 1))
                    if e < EXPERTS:
                        for u in range(2):
                            t = 2 * half_no + u
                            last = dve.scalar_tensor_tensor(
                                out=acc[p][0:R, t, :], in0=ps_y[half_no][0:R, u * C:(u + 1) * C],
                                scalar=comb[p][0:R, t, e:e + 1], in1=before[0:R, t, :],
                                op0=ALU.mult, op1=ALU.add)
                    else:
                        two = acc[p][0:R, 2 * half_no:2 * half_no + 2, :].rearrange("p t c -> p (t c)")
                        last = dve.scalar_tensor_tensor(out=two, in0=ps_y[half_no][0:R, 0:2 * C],
                                                        scalar=1.0 / (SA * SW), in1=two,
                                                        op0=ALU.mult, op1=ALU.add)
                    last.then_inc(acc_done, 1)

            first = Index(0, 0, 2, GROUPS_B)
            stats_of(first)
            normalise(first)
            yT_out(first)
            for part_no in range(3):
                route(first, part_no)

            def body(g):
                following = g.back(-1)
                for e in range(NE):
                    multiply(g, e)
                    if e > 0:
                        inner_rest(g, e - 1)
                    elif g.back(1).active():
                        inner_rest(g.back(1), NE - 1)
                    if e > 1:
                        accumulate(g, e - 2)
                    elif g.back(1).active():
                        accumulate(g.back(1), e + NE - 2)
                    if e < 2:
                        route(g, e + 3)
                    if following.active():
                        if e == 1:
                            stats_of(following)
                        if e == 2:
                            normalise(following)
                        if e == 4:
                            yT_out(following)
                        if e > 5:
                            route(following, e - 6)
                if not following.active():
                    inner_rest(g, NE - 1)
                    accumulate(g, NE - 2)
                    accumulate(g, NE - 1)
            run(dve.Fori, body)

        @block.gpsimd
        def _(pool):
            settled = sem("pool_settled_b")

            def rstds(g):
                R = rows_of(g)
                pool.wait_ge(bmv_done, g.times(T, T))
                settle(pool, settled)
                pool.tensor_scalar(bvareps[0:R], bmv[0:R, :, 1], EPS, None, ALU.add).then_inc(bve_done, 1)
                pool.wait_ge(bve_done, g.times(1, 1))
                pool.tensor_tensor(brstd[0:R], bvareps[0:R], minus_half[0:R], ALU.pow).then_inc(brstd_done, 1)

            rstds(Index(0, 0, 2, GROUPS_B))

            def body(g):
                if g.back(-1).active():
                    rstds(g.back(-1))
            run(pool.Fori, body)


def kernel(x, L0_tok_W_lin, L0_tok_b_lin, L0_tok_cls_token, L0_attn_qkv_weight, L0_attn_proj_weight,
           L0_ffn_gate_weight, L0_ffn_gate_bias, L0_ffn_w1, L0_ffn_w2, L0_ffn_w3, L0_ffn_sw1, L0_ffn_sw2,
           L0_ffn_sw3):
    import numpy as np
    import concourse.bacc as bacc
    from concourse.bass_utils import run_bass_kernel_spmd

    pixels = np.asarray(x).reshape(IMAGES, CHANNELS, GRID, PS, GRID, PS).transpose(0, 1, 3, 5, 2, 4)
    pixels = pixels.reshape(IMAGES, PCHUNKS, 128, PATCHES).transpose(0, 2, 1, 3)
    xp = np.zeros((IMAGES, 128, PCHUNKS, SLOTS), np.float32)
    xp[..., 0:TR] = pixels[..., 0:TR]
    xp[..., TR:SLOTS - 1] = pixels[..., TR - 1:PATCHES]

    def chunked(w, rows):
        w = np.asarray(w).T
        return np.ascontiguousarray(w.reshape(w.shape[0] // rows, rows, w.shape[1]).transpose(1, 0, 2))

    bias_cls = np.empty((TR, 2, C), np.float32)
    bias_cls[:] = np.asarray(L0_tok_b_lin)
    bias_cls[TR - 1, 1] = np.asarray(L0_tok_cls_token)[0]
    w1 = np.concatenate([np.asarray(L0_ffn_w1), np.asarray(L0_ffn_sw1)[None]])
    w3 = np.concatenate([np.asarray(L0_ffn_w3), np.asarray(L0_ffn_sw3)[None]])
    w2 = np.concatenate([np.asarray(L0_ffn_w2), np.asarray(L0_ffn_sw2)[None]])
    w13 = np.stack([w1, w3], 1).reshape(NE, 2, INTER, 2, KC).transpose(4, 3, 0, 1, 2)
    gate_bias = np.empty((128, LANES, EXPERTS), np.float32)
    gate_bias[:] = np.asarray(L0_ffn_gate_bias)

    def before(m):
        return np.ascontiguousarray(np.broadcast_to(np.tril(np.ones((m, m), np.float32), -1), (128, m, m)))

    arrays = {
        "xp": xp, "w_lin": chunked(L0_tok_W_lin, 128), "bias_cls": bias_cls,
        "w_qkv": chunked(L0_attn_qkv_weight, KC), "w_proj": chunked(L0_attn_proj_weight, KC),
        "w_gate": chunked(L0_ffn_gate_weight, KC), "gate_bias": gate_bias,
        "w13": np.ascontiguousarray(w13), "w2": np.ascontiguousarray(w2.transpose(2, 0, 1)),
        "ident": np.eye(128, dtype=np.float32), "before4": before(EGROUPS), "before8": before(EXPERTS),
    }
    nc = bacc.Bacc("TRN2", target_bir_lowering=False, num_devices=1)
    ins = [nc.dram_tensor(n, a.shape, F32, kind="ExternalInput").ap() for n, a in arrays.items()]
    out = nc.dram_tensor("out", (IMAGES, TOKENS, C), F32, kind="ExternalOutput").ap()
    vit_layer(nc, *ins, out)
    r = run_bass_kernel_spmd(nc, [arrays], core_ids=[0])
    return r.results[0]["out"]
```
